# Optimizing a Trainium2 kernel written in Bass

```python
import numpy as np
import jax
import jax.numpy as jnp

def _softmax(x, axis=-1):
    return jax.nn.softmax(x, axis=axis)

def _gelu(x):
    return jax.nn.gelu(x, approximate=True)

def _silu(x):
    return jax.nn.silu(x)

def _sigmoid(x):
    return jax.nn.sigmoid(x)

def _layernorm(x, axis=-1, eps=1e-05):
    m = jnp.mean(x, axis=axis, keepdims=True)
    v = jnp.var(x, axis=axis, keepdims=True)
    return (x - m) / jnp.sqrt(v + eps)

def _scatter_add(tgt, idx, src, axis=0):
    return tgt.at[idx].add(src)

def _segment_sum(src, seg, n):
    return jax.ops.segment_sum(src, seg, n)
kernel_name = 'mk_sandwich_d1_jaxref_r4_8b3aa0'

def setup_inputs(seed: int=0):
    np.random.seed(seed)
    _w = jnp.asarray

    def _L0_attn_setup():
        import jax, jax.numpy as jnp
        import numpy as np
        HEADS = 16

        def _binarize(W):
            alpha = jnp.mean(jnp.abs(W), axis=tuple(range(1, W.ndim)), keepdims=True)
            B = W + jax.lax.stop_gradient(jnp.sign(W) - W)
            return alpha * B

        def _binlinear(x, W, b):
            Wb = _binarize(W)
            return jnp.einsum('btc,oc->bto', x, Wb) + b
        key = jax.random.key(seed)
        ks = jax.random.split(key, 9)
        dim = 256
        B, T = (4, 512)
        inp = {'x': jax.random.normal(ks[0], (B, T, dim), jnp.float32), 'Wq': jax.random.normal(ks[1], (dim, dim), jnp.float32) * 0.02, 'bq': jax.random.normal(ks[2], (dim,), jnp.float32) * 0.02, 'Wk': jax.random.normal(ks[3], (dim, dim), jnp.float32) * 0.02, 'bk': jax.random.normal(ks[4], (dim,), jnp.float32) * 0.02, 'Wv': jax.random.normal(ks[5], (dim, dim), jnp.float32) * 0.02, 'bv': jax.random.normal(ks[6], (dim,), jnp.float32) * 0.02, 'Wp': jax.random.normal(ks[7], (dim, dim), jnp.float32) * 0.02, 'bp': jax.random.normal(ks[8], (dim,), jnp.float32) * 0.02}
        return inp
    _L0_attn_in = _L0_attn_setup()

    def _L0_ffn_setup():
        import jax, jax.numpy as jnp
        import numpy as np
        D_IN, D_HID = (256, 1024)

        def _ternary(key, shape):
            return jax.random.randint(key, shape, -1, 2).astype(jnp.float32)

        def _tlin(x, w, s):
            return jnp.einsum('bsi,oi->bso', x, w) * s
        key = jax.random.key(seed)
        ks = jax.random.split(key, 12)
        inv = lambda fan: 1.0 / np.sqrt(fan).astype(np.float32)
        return {'x': jax.random.normal(ks[0], (4, 512, D_IN), dtype=jnp.float32), 'w1_w': _ternary(ks[1], (D_HID, D_IN)), 'w1_s': jax.random.uniform(ks[2], (D_HID,), dtype=jnp.float32) * inv(D_IN), 'w2_w': _ternary(ks[3], (D_HID, D_IN)), 'w2_s': jax.random.uniform(ks[4], (D_HID,), dtype=jnp.float32) * inv(D_IN), 'h1_w': _ternary(ks[5], (D_HID, D_HID)), 'h1_s': jax.random.uniform(ks[6], (D_HID,), dtype=jnp.float32) * inv(D_HID), 'h2_w': _ternary(ks[7], (D_HID, D_HID)), 'h2_s': jax.random.uniform(ks[8], (D_HID,), dtype=jnp.float32) * inv(D_HID), 'w3_w': _ternary(ks[9], (D_IN, D_HID)), 'w3_s': jax.random.uniform(ks[10], (D_IN,), dtype=jnp.float32) * inv(D_HID)}
    _L0_ffn_in = _L0_ffn_setup()
    _d = {'L0_attn_x': _L0_attn_in['x'], 'L0_attn_Wq': _L0_attn_in['Wq'], 'L0_attn_bq': _L0_attn_in['bq'], 'L0_attn_Wk': _L0_attn_in['Wk'], 'L0_attn_bk': _L0_attn_in['bk'], 'L0_attn_Wv': _L0_attn_in['Wv'], 'L0_attn_bv': _L0_attn_in['bv'], 'L0_attn_Wp': _L0_attn_in['Wp'], 'L0_attn_bp': _L0_attn_in['bp'], 'L0_ffn_w1_w': _L0_ffn_in['w1_w'], 'L0_ffn_w1_s': _L0_ffn_in['w1_s'], 'L0_ffn_w2_w': _L0_ffn_in['w2_w'], 'L0_ffn_w2_s': _L0_ffn_in['w2_s'], 'L0_ffn_h1_w': _L0_ffn_in['h1_w'], 'L0_ffn_h1_s': _L0_ffn_in['h1_s'], 'L0_ffn_h2_w': _L0_ffn_in['h2_w'], 'L0_ffn_h2_s': _L0_ffn_in['h2_s'], 'L0_ffn_w3_w': _L0_ffn_in['w3_w'], 'L0_ffn_w3_s': _L0_ffn_in['w3_s']}
    _x0 = _d['L0_attn_x']
    _d['L0_attn_x'] = jax.random.normal(jax.random.fold_in(jax.random.key(seed), 1), (4, 1024, 256), dtype=_x0.dtype)
    del _x0
    return _d

def reference(L0_attn_x, L0_attn_Wq, L0_attn_bq, L0_attn_Wk, L0_attn_bk, L0_attn_Wv, L0_attn_bv, L0_attn_Wp, L0_attn_bp, L0_ffn_w1_w, L0_ffn_w1_s, L0_ffn_w2_w, L0_ffn_w2_s, L0_ffn_h1_w, L0_ffn_h1_s, L0_ffn_h2_w, L0_ffn_h2_s, L0_ffn_w3_w, L0_ffn_w3_s):

    def _L0_attn_ref(x, Wq, bq, Wk, bk, Wv, bv, Wp, bp):
        import jax, jax.numpy as jnp
        import numpy as np
        HEADS = 16

        def _binarize(W):
            alpha = jnp.mean(jnp.abs(W), axis=tuple(range(1, W.ndim)), keepdims=True)
            B = W + jax.lax.stop_gradient(jnp.sign(W) - W)
            return alpha * B

        def _binlinear(x, W, b):
            Wb = _binarize(W)
            return jnp.einsum('btc,oc->bto', x, Wb) + b
        B, T, C = x.shape
        H = HEADS
        Dh = C // H
        scale = Dh ** (-0.5)

        def split_heads(t):
            return t.reshape(B, T, H, Dh).transpose(0, 2, 1, 3)
        q = split_heads(_binlinear(x, Wq, bq))
        k = split_heads(_binlinear(x, Wk, bk))
        v = split_heads(_binlinear(x, Wv, bv))
        att = jnp.einsum('bhtd,bhsd->bhts', q, k) * scale
        att = jax.nn.softmax(att, axis=-1)
        y = jnp.einsum('bhts,bhsd->bhtd', att, v)
        y = y.transpose(0, 2, 1, 3).reshape(B, T, C)
        return _binlinear(y, Wp, bp)

    def _L0_ffn_ref(x, w1_w, w1_s, w2_w, w2_s, h1_w, h1_s, h2_w, h2_s, w3_w, w3_s):
        import jax, jax.numpy as jnp
        import numpy as np
        D_IN, D_HID = (256, 1024)

        def _ternary(key, shape):
            return jax.random.randint(key, shape, -1, 2).astype(jnp.float32)

        def _tlin(x, w, s):
            return jnp.einsum('bsi,oi->bso', x, w) * s
        h = jax.nn.silu(_tlin(x, w1_w, w1_s)) * _tlin(x, w2_w, w2_s)
        h = jax.nn.gelu(_tlin(h, h1_w, h1_s), approximate=False)
        h = jax.nn.gelu(_tlin(h, h2_w, h2_s), approximate=False)
        return _tlin(h, w3_w, w3_s)
    x = L0_attn_x
    x = x + _layernorm(_L0_attn_ref(_layernorm(x, axis=-1), L0_attn_Wq, L0_attn_bq, L0_attn_Wk, L0_attn_bk, L0_attn_Wv, L0_attn_bv, L0_attn_Wp, L0_attn_bp), axis=-1)
    x = x + _layernorm(_L0_ffn_ref(_layernorm(x, axis=-1), L0_ffn_w1_w, L0_ffn_w1_s, L0_ffn_w2_w, L0_ffn_w2_s, L0_ffn_h1_w, L0_ffn_h1_s, L0_ffn_h2_w, L0_ffn_h2_s, L0_ffn_w3_w, L0_ffn_w3_s), axis=-1)
    return x

_drawn_inputs = setup_inputs


def setup_inputs(seed=0):
    import zlib

    import numpy as np

    out = dict(_drawn_inputs(seed))
    spreads = {}
    factors = {'L0_attn_Wq': 5.113, 'L0_attn_bq': 8.0, 'L0_attn_Wk': 4.958, 'L0_attn_bk': 8.0}
    for name, (base, spread) in spreads.items():
        noise = np.random.default_rng([zlib.crc32(name.encode()), seed]).standard_normal(out[name].shape)
        drawn = base * np.exp(spread * noise) if base else spread * noise
        out[name] = jnp.asarray(drawn.astype(out[name].dtype))
    for name, factor in factors.items():
        out[name] = (out[name] * factor).astype(out[name].dtype)
    return out
```

```python
from contextlib import ExitStack

import concourse.bass as bass
from concourse import mybir

F32 = mybir.dt.float32
F32R = mybir.dt.float32r
BF16 = mybir.dt.bfloat16
I32 = mybir.dt.int32
ACT = mybir.ActivationFunctionType
ALU = mybir.AluOpType
AX = mybir.AxisListType

P = 128
BATCH, SEQ, DIM = 4, 1024, 256
HEADS, HEAD_DIM = 16, 16
HIDDEN = 1024
TOKENS = BATCH * SEQ
BLK = 512
BLOCKS = TOKENS // BLK
TILES = BLK // P
CT = DIM // P
HT = HIDDEN // P
QUAD = 4
QUADS = BATCH * HEADS // QUAD
ST = SEQ // P
QROWS = QUAD * HEAD_DIM
STACK = 6 * HEAD_DIM
STACK_M = STACK + 3
EPS = 1e-5
SCALE = HEAD_DIM ** -0.5
Q_PART = [0, 0, 1, 1, 0, 2]
K_PART = [0, 1, 0, 1, 2, 0]
W1_AT, W2_AT = 0, CT * HIDDEN
H1_AT = 2 * CT * HIDDEN
H2_AT = H1_AT + HT * HIDDEN
W3_AT = H2_AT + HT * HIDDEN
W_ALL = W3_AT + HT * DIM
S1_AT, S2_AT, SH1_AT, SH2_AT, S3_AT, S_ALL = 0, HT, 2 * HT, 3 * HT, 4 * HT, 4 * HT + CT


def layer(nc, x, attn_w, attn_wT, attn_b, ffn_w, ffn_s, out):
    dram = {}

    def scratch(name, shape, dt):
        dram[name] = nc.dram_tensor(name, shape, dt, kind="Internal").ap()
        return dram[name]

    q_scr = scratch("q_scr", (3, BATCH * DIM, SEQ), BF16)
    k_scr = scratch("k_scr", (3, BATCH * DIM, SEQ), BF16)
    v_scr = scratch("v_scr", (QUADS * P, ST, P), F32)
    m_scr = scratch("m_scr", (3, BATCH * HEADS, SEQ), BF16)
    y_scr = scratch("y_scr", (QUADS * P, SEQ), F32)
    w_scr = scratch("w_scr", (P, W_ALL), F32)

    with ExitStack() as keep:
        def sb(name, shape, dt, stack=keep):
            return stack.enter_context(nc.sbuf_tensor(name, shape, dt))

        def sem(name, stack=keep):
            return stack.enter_context(nc.semaphore(name))

        W = sb("W", [P, W_ALL], F32R)
        signs = sb("signs", [P, 4, CT, DIM], F32R)
        alpha = sb("alpha", [P, 4 * CT], F32)
        bias = sb("bias", [P, 4 * CT], F32)
        scales = sb("scales", [P, S_ALL], F32)
        ident = sb("ident", [P, P], F32)
        spread = sb("spread", [HEADS, CT, P], F32)
        eps = sb("eps", [P, 1], F32)
        w_in_scr = sem("w_in_scr")
        w_loaded = sem("w_loaded")

        setup(nc, attn_w, attn_wT, attn_b, ffn_w, ffn_s, w_scr, W, signs, alpha, bias, scales,
              ident, spread, eps, w_in_scr)
        project(nc, x, signs, alpha, bias, ident, eps, q_scr, k_scr, v_scr, w_scr, W, w_in_scr, w_loaded)
        row_maxima(nc, q_scr, k_scr, m_scr, ident)
        attention(nc, q_scr, k_scr, v_scr, m_scr, y_scr)
        tail_ffn(nc, x, y_scr, W, signs, alpha, bias, scales, ident, spread, eps, out, w_loaded)


def setup(nc, attn_w, attn_wT, attn_b, ffn_w, ffn_s, w_scr, W, signs, alpha, bias, scales,
          ident, spread, eps, w_in_scr):
    with (nc.sbuf_tensor("w_nat", [P, 4 * CT, DIM], F32) as w_nat,
          nc.sbuf_tensor("w_tr", [P, 4, CT, DIM], F32) as w_tr,
          nc.sbuf_tensor("abs_sum", [P, 4 * CT], F32) as abs_sum,
          nc.semaphore("nat_loaded") as nat_loaded, nc.semaphore("tr_loaded") as tr_loaded,
          nc.semaphore("small_loaded") as small_loaded, nc.semaphore("filled") as filled,
          nc.semaphore("summed") as summed, nc.Block() as block):

        @block.sync
        def _(sp):
            sp.dma_start(w_tr[:, :, :, :], attn_wT).then_inc(tr_loaded, 16)
            sp.dma_start(w_nat[:, :, :], attn_w).then_inc(nat_loaded, 16)
            sp.dma_start(bias[:, :], attn_b).then_inc(small_loaded, 16)
            sp.dma_start(scales[:, :], ffn_s).then_inc(small_loaded, 16)
            sp.dma_start(w_scr, ffn_w).then_inc(w_in_scr, 16)
            sp.wait_ge(small_loaded, 32)

        @block.scalar
        def _(act):
            act.wait_ge(tr_loaded, 16)
            act.activation(signs[:, :, :, :], w_tr[:, :, :, :], ACT.Sign)

        @block.vector
        def _(dve):
            dve.memset(eps[:, :], EPS)
            dve.wait_ge(nat_loaded, 16)
            dve.tensor_reduce(abs_sum[:, :], w_nat[:, :, :], AX.X, ALU.add,
                              apply_absolute_value=True).then_inc(summed, 1)
            dve.wait_ge(summed, 1)
            dve.tensor_scalar(alpha[:, :], abs_sum[:, :], 1.0 / DIM, None, ALU.mult)

        @block.gpsimd
        def _(pool):
            pool.memset(ident[:, :], 0.0).then_inc(filled, 1)
            pool.memset(spread[:, :, :], 1.0).then_inc(filled, 1)
            pool.wait_ge(filled, 2)
            pool.affine_select(out=ident[:, :], in_=ident[:, :], compare_op=ALU.not_equal, fill=1.0,
                               base=0, pattern=[[-1, P]], channel_multiplier=1)
            pool.affine_select(out=spread[:, :, :], in_=spread[:, :, :], compare_op=ALU.is_ge, fill=0.0,
                               base=0, pattern=[[P, CT], [1, P]],
                               channel_multiplier=-HEAD_DIM).then_inc(filled, 1)
            pool.wait_ge(filled, 3)
            pool.affine_select(out=spread[:, :, :], in_=spread[:, :, :], compare_op=ALU.is_ge, fill=0.0,
                               base=HEAD_DIM - 1, pattern=[[-P, CT], [-1, P]],
                               channel_multiplier=HEAD_DIM)


def project(nc, x, signs, alpha, bias, ident, eps, q_scr, k_scr, v_scr, w_scr, W, w_in_scr, w_loaded):
    QK = 2 * CT
    x_blk = x.rearrange("b (h t p) c -> (b h) p t c", p=P, t=TILES)
    q_rows = q_scr.rearrange("s (b c p) t -> s b p c t", p=P, c=CT)
    k_rows = k_scr.rearrange("s (b c p) t -> s b p c t", p=P, c=CT)
    v_rows = v_scr.rearrange("(b q p) s n -> b q p s n", p=P, q=HEADS // QUAD)
    with ExitStack() as ctx:
        def sb(name, shape, dt):
            return ctx.enter_context(nc.sbuf_tensor(name, shape, dt))

        def sem(name):
            return ctx.enter_context(nc.semaphore(name))

        x_in = [sb(f"x_in{u}", [P, TILES, DIM], F32) for u in range(2)]
        x_norm = [sb(f"x_norm{u}", [P, TILES, DIM], F32) for u in range(2)]
        x_hi = [sb(f"x_hi{u}", [P, CT, BLK], F32R) for u in range(2)]
        x_lo = [sb(f"x_lo{u}", [P, CT, BLK], F32R) for u in range(2)]
        qkv = sb("qkv", [P, 3 * CT, BLK], F32)
        rest = sb("rest", [P, QK, BLK], F32)
        part = [[sb(f"part{s}{u}", [P, QK, BLK], BF16) for u in range(2)] for s in range(3)]
        v_aug = [sb(f"v_aug{u}", [P, TILES, HEADS, 2 * HEAD_DIM], F32) for u in range(2)]
        stats = sb("stats", [P, TILES, 6], F32)
        mean_var = sb("mean_var", [P, TILES, 2], F32)
        std = sb("std", [P, TILES], F32)
        rstd = sb("rstd", [P, TILES], F32)
        xT_ps = ctx.enter_context(nc.psum_tensor("xT_ps", [P, CT, BLK], F32))
        qkv_ps = ctx.enter_context(nc.psum_tensor("qkv_ps", [P, 3 * CT, BLK], F32))
        vT_ps = qkv_ps[:, 0:2, :].rearrange("p a (t c) -> p (a t) c", c=DIM)

        x_loaded = [sem(f"x_loaded{u}") for u in range(2)]
        stats_done = sem("stats_done")
        stats_seen = sem("stats_seen")
        var_done = sem("var_done")
        std_done = sem("std_done")
        rstd_done = sem("rstd_done")
        norm_done = sem("norm_done")
        xT_done = sem("xT_done")
        hi_done = sem("hi_done")
        lo_done = sem("lo_done")
        qkv_done = sem("qkv_done")
        qk_copied = sem("qk_copied")
        v_copied = sem("v_copied")
        vT_done = sem("vT_done")
        aug_done = sem("aug_done")
        high_done = sem("high_done")
        rest_done = sem("rest_done")
        mid_done = sem("mid_done")
        low_done = sem("low_done")
        aug_set = sem("aug_set")
        stored = [sem(f"stored{u}") for u in range(2)]
        STORES = 3 * 2 + HEADS // QUAD
        MT = 3 * CT

        block = ctx.enter_context(nc.Block())


        def blocks(eng, first, body):
            first(0, 0, 0)
            with eng.Fori(0, BATCH - 1) as b:
                body((b, 0, 2 * b), (b, 1, 2 * b + 1))
                body((b, 1, 2 * b + 1), (b + 1, 0, 2 * b + 2))
            b = BATCH - 1
            body((b, 0, 2 * b), (b, 1, 2 * b + 1))
            body((b, 1, 2 * b + 1), None)

        @block.sync
        def _(sp):
            def load(n, u):
                sp.dma_start(x_in[u][:, :, :], x_blk[n]).then_inc(x_loaded[u], 16)

            def first(b, u, n):
                load(0, 0)
                load(1, 1)
                sp.wait_ge(w_in_scr, 16)
                sp.dma_start(W[:, :].bitcast(F32), w_scr).then_inc(w_loaded, 16)

            def body(b, last):
                for u in range(2):
                    n = 2 * b + u
                    t0 = u * BLK
                    if not last:
                        sp.wait_ge(norm_done, TILES * (n + 1))
                        load(n + 2, u)
                    for s, (done, credit) in enumerate(((high_done, 0), (mid_done, 0), (low_done, 1))):
                        sp.wait_ge(done, credit + n + 1)
                        for scr, m in ((q_rows, 0), (k_rows, CT)):
                            sp.dma_start(scr[s, b, :, :, t0:t0 + BLK],
                                         part[s][u][:, m:m + CT, :]).then_inc(stored[u], 16)
                    sp.wait_ge(aug_done, n + 1)
                    for q in range(HEADS // QUAD):
                        sp.dma_start(v_rows[b, q, :, TILES * u:TILES * (u + 1), :],
                                     v_aug[u][:, :, QUAD * q:QUAD * (q + 1), :]
                                     .rearrange("p t h n -> p t (h n)")).then_inc(stored[u], 16)

            first(0, 0, 0)
            with sp.Fori(0, BATCH - 1) as b:
                body(b, False)
            body(BATCH - 1, True)
            for u in range(2):
                sp.wait_ge(stored[u], 16 * (STORES * BATCH + 1))
            sp.wait_ge(w_loaded, 16)

        @block.vector
        def _(dve):
            def normalise(b, u, n):
                dve.wait_ge(x_loaded[u], 16 * (b + 1))
                for t in range(TILES):
                    dve.bn_stats(stats[:, t, :], x_in[u][:, t, :]).then_inc(stats_done, 1)
                dve.wait_ge(stats_done, TILES * (n + 1))
                dve.sem_inc(stats_seen, 1)
                for t in range(TILES):
                    dve.bn_aggr(mean_var[:, t, :], stats[:, t, :]).then_inc(var_done, 1)
                dve.wait_ge(std_done, n + 1)
                dve.reciprocal(rstd[:, :], std[:, :]).then_inc(rstd_done, 1)
                dve.wait_ge(rstd_done, n + 1)
                dve.wait_ge(xT_done, n)
                for t in range(TILES):
                    dve.tensor_scalar(x_norm[u][:, t, :], x_in[u][:, t, :], mean_var[:, t, 0:1],
                                      rstd[:, t:t + 1], ALU.subtract, ALU.mult).then_inc(norm_done, 1)

            def low_of_x(b, u, n):
                dve.wait_ge(hi_done, n + 1)
                dve.tensor_tensor(x_lo[u][:, :, :], xT_ps[:, :, :], x_hi[u][:, :, :].bitcast(F32),
                                  ALU.subtract).then_inc(lo_done, 1)

            def parts(b, u, n):
                dve.wait_ge(qk_copied, QK * (n + 1))
                dve.wait_ge(stored[u], 16 * (STORES * b + 1))
                dve.tensor_copy(part[0][u][:, :, :], qkv[:, 0:QK, :]).then_inc(high_done, 1)
                dve.wait_ge(high_done, n + 1)
                dve.wait_ge(low_done, n + 1)
                dve.tensor_tensor(rest[:, :, :], qkv[:, 0:QK, :], part[0][u][:, :, :],
                                  ALU.subtract).then_inc(rest_done, 1)
                dve.wait_ge(rest_done, n + 2)
                dve.tensor_copy(part[1][u][:, :, :], rest[:, :, :]).then_inc(mid_done, 1)

            def first(b, u, n):
                normalise(b, u, n)
                low_of_x(b, u, n)

            def body(now, ahead):
                if ahead:
                    normalise(*ahead)
                parts(*now)
                if ahead:
                    low_of_x(*ahead)

            blocks(dve, first, body)

        @block.gpsimd
        def _(pool):
            pool.sem_inc(low_done, 1)
            pool.sem_inc(rest_done, 1)
            pool.sem_inc(vT_done, 1)
            for u in range(2):
                pool.sem_inc(stored[u], 16)
            for u in range(2):
                pool.memset(v_aug[u][:, :, :, HEAD_DIM:HEAD_DIM + 1], 1.0).then_inc(aug_set, 1)
                pool.memset(v_aug[u][:, :, :, HEAD_DIM + 1:], 0.0).then_inc(aug_set, 1)
            with pool.Fori(0, BATCH) as b:
                for u in range(2):
                    n = 2 * b + u
                    pool.wait_ge(mid_done, n + 1)
                    pool.wait_ge(stored[u], 16 * (STORES * b + 1))
                    pool.tensor_tensor(part[2][u][:, :, :], rest[:, :, :], part[1][u][:, :, :],
                                       ALU.subtract).then_inc(low_done, 1)

        @block.scalar
        def _(act):
            def std_of(b, u, n):
                act.wait_ge(var_done, TILES * (n + 1))
                act.activation(std[:, :], mean_var[:, :, 1], ACT.Sqrt, bias=eps[:, :]).then_inc(std_done, 1)

            def high_of_x(b, u, n):
                act.wait_ge(xT_done, n + 1)
                act.activation(x_hi[u][:, :, :], xT_ps[:, :, :], ACT.Copy).then_inc(hi_done, 1)

            def copy_qkv(b, u, n):
                act.wait_ge(rest_done, n + 1)
                for m in range(MT):
                    act.wait_ge(qkv_done, MT * n + m + 1)
                    if m == QK:
                        act.wait_ge(vT_done, n + 1)
                    act.activation(qkv[:, m, :], qkv_ps[:, m, :], ACT.Identity, bias=bias[:, m:m + 1],
                                   scale=alpha[:, m:m + 1]).then_inc(qk_copied if m < QK else v_copied, 1)

            def copy_v(b, u, n):
                act.wait_ge(vT_done, n + 2)
                act.wait_ge(stored[u], 16 * (STORES * b + 1))
                act.activation(v_aug[u][:, :, :, 0:HEAD_DIM], vT_ps.rearrange("p t (h d) -> p t h d", d=HEAD_DIM),
                               ACT.Copy).then_inc(aug_done, 1)

            def first(b, u, n):
                std_of(b, u, n)
                high_of_x(b, u, n)

            def body(now, ahead):
                if ahead:
                    std_of(*ahead)
                copy_qkv(*now)
                copy_v(*now)
                if ahead:
                    high_of_x(*ahead)

            blocks(act, first, body)

        @block.tensor
        def _(pe):
            def turn_x(b, u, n):
                pe.wait_ge(norm_done, TILES * (n + 1))
                pe.wait_ge(lo_done, n)
                for t in range(TILES):
                    for c in range(CT):
                        i = pe.transpose(xT_ps[:, c, t * P:(t + 1) * P],
                                         x_norm[u][:, t, c * P:(c + 1) * P], ident[:, :])
                i.then_inc(xT_done, 1)

            def project_x(b, u, n):
                pe.wait_ge(lo_done, n + 1)
                pe.wait_ge(aug_done, n)
                for m in range(MT):
                    for c in range(CT):
                        w = signs[:, m // CT, c, (m % CT) * P:(m % CT + 1) * P]
                        pe.matmul(qkv_ps[:, m, :], w, x_hi[u][:, c, :], start=(c == 0), stop=False)
                        i = pe.matmul(qkv_ps[:, m, :], w, x_lo[u][:, c, :], start=False, stop=(c == CT - 1))
                    i.then_inc(qkv_done, 1)

            def turn_v(b, u, n):
                pe.wait_ge(qk_copied, QK * (n + 1))
                pe.wait_ge(v_copied, CT * (n + 1))
                for t in range(TILES):
                    for c in range(CT):
                        i = pe.transpose(vT_ps[:, t, c * P:(c + 1) * P],
                                         qkv[:, QK + c, t * P:(t + 1) * P], ident[:, :])
                i.then_inc(vT_done, 1)

            def first(b, u, n):
                turn_x(b, u, n)
                project_x(b, u, n)

            def body(now, ahead):
                if ahead:
                    turn_x(*ahead)
                turn_v(*now)
                if ahead:
                    project_x(*ahead)

            blocks(pe, first, body)


def row_maxima(nc, q_scr, k_scr, m_scr, ident):
    rows = m_scr.rearrange("s h (i p) -> (h i) s p", p=P)
    with ExitStack() as ctx:
        def sb(name, shape, dt):
            return ctx.enter_context(nc.sbuf_tensor(name, shape, dt))

        def sem(name):
            return ctx.enter_context(nc.semaphore(name))

        q_st = sb("q_st", [STACK, QUAD, SEQ], BF16)
        k_st = sb("k_st", [STACK, QUAD, SEQ], BF16)
        top = sb("top", [P, QUAD * ST], F32)
        neg = sb("neg", [QUAD * ST, P], F32)
        left = sb("left", [QUAD * ST, P], F32)
        left2 = sb("left2", [QUAD * ST, P], F32)
        m_part = sb("m_part", [QUAD * ST, 3, P], BF16)
        s_ps = [ctx.enter_context(nc.psum_tensor(f"s_ps{i}", [P, SEQ], F32)) for i in range(3)]
        t_ps = ctx.enter_context(nc.psum_tensor("t_ps", [QUAD * ST, P], F32))
        loaded = sem("mx_loaded")
        scored = sem("mx_scored")
        reduced = sem("mx_reduced")
        turned = sem("mx_turned")
        stepped = sem("mx_stepped")
        stored = sem("mx_stored")
        block = ctx.enter_context(nc.Block())
        N = QUAD * ST

        @block.sync
        def _(sp):
            with sp.Fori(0, QUADS) as g:
                sp.wait_ge(turned, g + 1)
                for i in range(6):
                    at = slice(i * HEAD_DIM, (i + 1) * HEAD_DIM)
                    for st, scr, s in ((q_st, q_scr, Q_PART[i]), (k_st, k_scr, K_PART[i])):
                        sp.dma_start(st[at, :, :], scr[s, bass.ds(g * QROWS, QROWS), :]
                                     .rearrange("(j d) t -> d j t", d=HEAD_DIM)).then_inc(loaded, 16)
                sp.wait_ge(stepped, 6 * (g + 1) + 1)
                sp.dma_start(rows[bass.ds(g * N, N), :, :], m_part[:, :, :]).then_inc(stored, 16)
            sp.wait_ge(stored, 16 * (QUADS + 1))

        @block.scalar
        def _(act):
            for s in (turned, stepped, reduced):
                act.sem_inc(s, 1)
            act.sem_inc(stored, 16)

        @block.tensor
        def _(pe):
            with pe.Fori(0, QUADS) as g:
                pe.wait_ge(loaded, 16 * 12 * (g + 1))
                for a in range(N):
                    j, t = divmod(a, ST)
                    if a >= 3:
                        pe.wait_ge(reduced, g * N + a - 1)
                    else:
                        pe.wait_ge(reduced, g * N + 1)
                    for h in range(2):
                        i = pe.matmul(s_ps[a % 3][:, h * BLK:(h + 1) * BLK], q_st[:, j, t * P:(t + 1) * P],
                                      k_st[:, j, h * BLK:(h + 1) * BLK], start=True, stop=True)
                    i.then_inc(scored, 1)
                pe.wait_ge(reduced, (g + 1) * N + 1)
                pe.wait_ge(stepped, 6 * g + 1)
                pe.transpose(t_ps[:, :], top[:, :], ident[:, :]).then_inc(turned, 1)

        @block.vector
        def _(dve):
            with dve.Fori(0, QUADS) as g:
                dve.wait_ge(turned, g + 1)
                for a in range(N):
                    dve.wait_ge(scored, g * N + a + 1)
                    dve.tensor_reduce(top[:, a:a + 1], s_ps[a % 3][:, :], AX.X, ALU.max).then_inc(reduced, 1)
                dve.wait_ge(turned, g + 2)
                dve.wait_ge(stored, 16 * (g + 1))
                k = 6 * g + 1
                dve.tensor_scalar(neg[:, :], t_ps[:, :], -1.0, None, ALU.mult).then_inc(stepped, 1)
                dve.wait_ge(stepped, k + 1)
                dve.tensor_copy(m_part[:, 0, :], neg[:, :]).then_inc(stepped, 1)
                dve.wait_ge(stepped, k + 2)
                dve.tensor_tensor(left[:, :], neg[:, :], m_part[:, 0, :], ALU.subtract).then_inc(stepped, 1)
                dve.wait_ge(stepped, k + 3)
                dve.tensor_copy(m_part[:, 1, :], left[:, :]).then_inc(stepped, 1)
                dve.wait_ge(stepped, k + 4)
                dve.tensor_tensor(left2[:, :], left[:, :], m_part[:, 1, :], ALU.subtract).then_inc(stepped, 1)
                dve.wait_ge(stepped, k + 5)
                dve.tensor_copy(m_part[:, 2, :], left2[:, :]).then_inc(stepped, 1)


def attention(nc, q_scr, k_scr, v_scr, m_scr, y_scr):
    with ExitStack() as ctx:
        def sb(name, shape, dt):
            return ctx.enter_context(nc.sbuf_tensor(name, shape, dt))

        def sem(name):
            return ctx.enter_context(nc.semaphore(name))

        q_st = [sb(f"q_st{u}", [STACK_M, QUAD, SEQ], BF16) for u in range(2)]
        k_st = [sb(f"k_st{u}", [STACK_M, QUAD, SEQ], BF16) for u in range(2)]
        v_st = [sb(f"v_st{u}", [P, ST, P], F32) for u in range(2)]
        probs = [[sb(f"probs{w}{j}", [P, SEQ], F32) for j in range(QUAD)] for w in range(2)]
        y_sb = [sb(f"y_sb{u}", [P, SEQ], F32) for u in range(2)]
        s_ps = [ctx.enter_context(nc.psum_tensor(f"sc_ps{i}", [P, SEQ], F32)) for i in range(3)]
        y_ps = ctx.enter_context(nc.psum_tensor("y_ps", [P, SEQ], F32))
        loaded = [sem(f"loaded{u}") for u in range(2)]
        ones_set = sem("ones_set")
        scored = sem("scored")
        probs_ready = sem("probs_ready")
        pv_done = sem("pv_done")
        y_copied = sem("y_copied")
        y_stored = [sem(f"y_stored{u}") for u in range(2)]
        LOADS = 6 * 2 + 1 + 1
        N = QUAD * ST
        block = ctx.enter_context(nc.Block())

        @block.sync
        def _(sp):
            def load(g, u):
                for i in range(6):
                    at = slice(i * HEAD_DIM, (i + 1) * HEAD_DIM)
                    for st, scr, s in ((q_st, q_scr, Q_PART[i]), (k_st, k_scr, K_PART[i])):
                        sp.dma_start(st[u][at, :, :], scr[s, bass.ds(g * QROWS, QROWS), :]
                                     .rearrange("(j d) t -> d j t", d=HEAD_DIM)).then_inc(loaded[u], 16)
                sp.dma_start(q_st[u][STACK:STACK_M, :, :],
                             m_scr[:, bass.ds(g * QUAD, QUAD), :]).then_inc(loaded[u], 16)
                sp.dma_start(v_st[u][:, :, :], v_scr[bass.ds(g * P, P), :, :]).then_inc(loaded[u], 16)

            def body(h, last):
                for u in range(2):
                    g = 2 * h + u
                    sp.wait_ge(y_copied, g + 2)
                    sp.dma_start(y_scr[bass.ds(g * P, P), :], y_sb[u][:, :]).then_inc(y_stored[u], 16)
                    if not last:
                        load(g + 2, u)

            load(0, 0)
            load(1, 1)
            with sp.Fori(0, QUADS // 2 - 1) as h:
                body(h, False)
            body(QUADS // 2 - 1, True)
            for u in range(2):
                sp.wait_ge(y_stored[u], 16 * (QUADS // 2 + 1))

        @block.gpsimd
        def _(pool):
            pool.sem_inc(y_copied, 1)
            for u in range(2):
                pool.sem_inc(y_stored[u], 16)
            for u in range(2):
                pool.memset(k_st[u][STACK:STACK_M, :, :], 1.0).then_inc(ones_set, 1)

        @block.tensor
        def _(pe):
            def pv(g, u, s):
                pe.wait_ge(probs_ready, 3 + g * N + QUAD * (s + 1))
                for tb in range(2):
                    for j in range(QUAD):
                        i = pe.matmul(y_ps[32 * j:32 * (j + 1), tb * BLK:(tb + 1) * BLK],
                                      v_st[u][:, s, 32 * j:32 * (j + 1)],
                                      probs[s % 2][j][:, tb * BLK:(tb + 1) * BLK],
                                      start=(s == 0), stop=(s == ST - 1), tile_position=(0, 32 * j))
                i.then_inc(pv_done, 1)

            pe.wait_ge(ones_set, 2)
            with pe.Fori(0, QUADS // 2) as h:
                for u in range(2):
                    g = 2 * h + u
                    pe.wait_ge(loaded[u], 16 * LOADS * (h + 1))
                    for s in range(ST):
                        for j in range(QUAD):
                            a = s * QUAD + j
                            pe.wait_ge(probs_ready, g * N + ((2, 3, 1)[a] if a < 3 else a + 1))
                            for tb in range(2):
                                i = pe.matmul(s_ps[a % 3][:, tb * BLK:(tb + 1) * BLK],
                                              k_st[u][:, j, s * P:(s + 1) * P],
                                              q_st[u][:, j, tb * BLK:(tb + 1) * BLK], start=True, stop=True)
                            i.then_inc(scored, 1)
                        if s == 1:
                            pe.wait_ge(y_copied, g + 1)
                        if s >= 1:
                            pv(g, u, s - 1)
                    pv(g, u, ST - 1)

        @block.scalar
        def _(act):
            act.sem_inc(pv_done, 2)
            act.sem_inc(probs_ready, 3)
            with act.Fori(0, QUADS // 2) as h:
                for u in range(2):
                    g = 2 * h + u
                    for s in range(ST):
                        act.wait_ge(pv_done, g * ST + s + 1)
                        for j in range(QUAD):
                            a = s * QUAD + j
                            act.wait_ge(scored, g * N + a + 1)
                            act.activation(probs[s % 2][j][:, :], s_ps[a % 3][:, :], ACT.Exp,
                                           scale=SCALE).then_inc(probs_ready, 1)

        @block.vector
        def _(dve):
            with dve.Fori(0, QUADS // 2) as h:
                for u in range(2):
                    g = 2 * h + u
                    dve.wait_ge(pv_done, 2 + (g + 1) * ST)
                    dve.wait_ge(y_stored[u], 16 * (h + 1))
                    dve.tensor_copy(y_sb[u][:, :], y_ps[:, :]).then_inc(y_copied, 1)


def tail_ffn(nc, x, y_scr, W, signs, alpha, bias, scales, ident, spread, eps, out, w_loaded):
    x_blk = x.rearrange("b (h t p) c -> (b h) p t c", p=P, t=TILES)
    o_blk = out.rearrange("b (h t p) c -> (b h) p t c", p=P, t=TILES)
    y_blk = y_scr.rearrange("(b c a d) t -> b c a d t", b=BATCH, c=CT, d=2 * HEAD_DIM)
    y_heads = y_scr.rearrange("(b h d) t -> b h d t", b=BATCH, d=2 * HEAD_DIM)
    with ExitStack() as ctx:
        def sb(name, shape, dt):
            return ctx.enter_context(nc.sbuf_tensor(name, shape, dt))

        def sem(name):
            return ctx.enter_context(nc.semaphore(name))

        y = sb("y", [P, CT, BLK], F32)
        sums = sb("sums", [HEADS, BLK], F32)
        rsum = sb("rsum", [HEADS, BLK], F32)
        zn = sb("zn", [P, TILES, DIM], F32)
        x1 = [sb(f"x1_{u}", [P, TILES, DIM], F32) for u in range(2)]
        x2_hi = sb("x2_hi", [P, CT, BLK], F32R)
        x2_lo = sb("x2_lo", [P, CT, BLK], F32R)
        y_hi, y_lo = x2_hi, x2_lo
        z = y
        h_hi = [sb(f"h_hi{a}", [P, HT, BLK], F32R) for a in range(2)]
        h_lo = [sb(f"h_lo{a}", [P, HT, BLK], F32R) for a in range(2)]
        gate = [sb(f"gate{a}", [P, BLK], F32) for a in range(3)]
        hid = [sb(f"hid{a}", [P, BLK], F32) for a in range(3)]
        oT = sb("oT", [P, CT, BLK], F32)
        o_sb = zn
        stats = sb("ln_stats", [P, TILES, 6], F32)
        mean_var = sb("ln_mean_var", [P, TILES, 2], F32)
        std = sb("ln_std", [P, TILES], F32)
        rstd = sb("ln_rstd", [P, TILES], F32)
        BANKS = 6
        bank = [ctx.enter_context(nc.psum_tensor(f"ffn_ps{a}", [P, BLK], F32)) for a in range(BANKS)]
        side = ctx.enter_context(nc.psum_tensor("side_ps", [P, CT, BLK], F32))
        side_t = side[:, :, :].rearrange("p a (t c) -> p (a t) c", c=DIM)

        tail_loaded = sem("tail_loaded")
        rsum_done = sem("rsum_done")
        spread_done = sem("spread_done")
        y_done = sem("y_done")
        y_hi_done = sem("y_hi_done")
        y_lo_done = sem("y_lo_done")
        proj_done = sem("proj_done")
        z_copied = sem("z_copied")
        zT_done = sem("zT_done")
        zn_done = sem("zn_done")
        x1_done = sem("x1_done")
        x1n_done = sem("x1n_done")
        x2T_done = sem("x2T_done")
        x2_hi_done = sem("x2_hi_done")
        x2_lo_done = sem("x2_lo_done")
        ln_stats_done = sem("ln_stats_done")
        ln_stats_seen = sem("ln_stats_seen")
        ln_var_done = sem("ln_var_done")
        ln_std_done = sem("ln_std_done")
        ln_rstd_done = sem("ln_rstd_done")
        tile_done = sem("tile_done")
        gate_done = sem("gate_done")
        prod_done = sem("prod_done")
        hi1_done = sem("hi1_done")
        gelu_done = sem("gelu_done")
        hi2_done = sem("hi2_done")
        h_lo_done = sem("h_lo_done")
        oT_copied = sem("oT_copied")
        oT_turned = sem("oT_turned")
        o_norm = sem("o_norm")
        o_done = sem("o_done")
        o_stored = sem("o_stored")

        kinds = ["gate", "prod"] * HT + ["gelu"] * (2 * HT) + ["out"] * CT
        NT = len(kinds)
        reader = {"gate": gate_done, "prod": prod_done, "gelu": gelu_done, "out": oT_copied}
        per_block = {k: kinds.count(k) for k in reader}
        L2_AT, L3_AT, OUT_AT = 2 * HT, 3 * HT, 4 * HT

        def bank_of(t):
            return bank[t % BANKS]

        def wait_bank(pe, i, t):
            if t >= BANKS:
                before, blk = t - BANKS, i
            else:
                before, blk = max(p for p in range(NT) if p % BANKS == t), i - 1
                if isinstance(i, int) and i == 0:
                    return
            k = kinds[before]
            pe.wait_ge(reader[k], per_block[k] * blk + kinds[:before + 1].count(k))

        def ln_z(t):
            return 3 * t - 1 if not isinstance(t, int) or t else 0

        def ln_x1(t):
            return 3 * t if not isinstance(t, int) or t else 1

        def ln_out(f):
            return 3 * f + 4 if not isinstance(f, int) or f < BLOCKS - 1 else 3 * f + 2

        block = ctx.enter_context(nc.Block())

        def blocks(eng, first, step, end):
            first()
            step(0, 0, (0, 1), None)
            with eng.Fori(0, BATCH - 1) as b:
                step(2 * b + 1, 1, (b + 1, 0), (b, 0))
                step(2 * b + 2, 0, (b + 1, 1), (b, 1))
            step(BLOCKS - 1, 1, None, (BATCH - 1, 0))
            end()

        @block.sync
        def _(sp):
            def load_tail(t, b, u):
                sp.wait_ge(zT_done, t)
                if not isinstance(t, int) or t >= 2:
                    sp.wait_ge(o_done, t - 1)
                for c in range(CT):
                    sp.dma_start(y[:, c, :], y_blk[b, c, :, 0:HEAD_DIM, u * BLK:(u + 1) * BLK])\
                        .then_inc(tail_loaded, 16)
                sp.dma_start(sums[:, :], y_heads[b, :, HEAD_DIM, u * BLK:(u + 1) * BLK]).then_inc(tail_loaded, 16)
                sp.dma_start(x1[u][:, :, :], x_blk[t]).then_inc(tail_loaded, 16)

            def store(f):
                sp.wait_ge(o_done, f + 1)
                sp.dma_start(o_blk[f], o_sb[:, :, :]).then_inc(o_stored, 16)

            def first():
                load_tail(0, 0, 0)
                load_tail(1, 0, 1)

            def step(i, u, ahead, behind):
                if behind:
                    store(i - 1)
                if ahead and not (isinstance(i, int) and i == 0):
                    load_tail(i + 1, *ahead)

            blocks(sp, first, step, lambda: store(BLOCKS - 1))
            sp.wait_ge(o_stored, 16 * BLOCKS)

        @block.tensor
        def _(pe):
            def spread_sums(t):
                pe.wait_ge(rsum_done, t + 1)
                pe.wait_ge(x2_lo_done, t)
                for c in range(CT):
                    i = pe.matmul(side[:, c, :], spread[:, c, :], rsum[:, :], start=True, stop=True)
                i.then_inc(spread_done, 1)

            def project_y(t):
                pe.wait_ge(y_hi_done, t + 1)
                pe.wait_ge(y_lo_done, t + 1)
                for m in range(CT):
                    for c in range(CT):
                        w = signs[:, 3, c, m * P:(m + 1) * P]
                        pe.matmul(side[:, m, :], w, y_hi[:, c, :], start=(c == 0), stop=False)
                        i = pe.matmul(side[:, m, :], w, y_lo[:, c, :], start=False, stop=(c == CT - 1))
                i.then_inc(proj_done, 1)

            def turn_back(src, copied, turned):
                pe.wait_ge(*copied)
                for t in range(TILES):
                    for c in range(CT):
                        i = pe.transpose(side_t[:, t, c * P:(c + 1) * P], src[:, c, t * P:(t + 1) * P], ident[:, :])
                i.then_inc(turned, 1)

            def turn_z(t):
                turn_back(z, (z_copied, t + 1), zT_done)

            def turn_x1(t):
                pe.wait_ge(x1n_done, TILES * (t + 1))
                for a in range(TILES):
                    for c in range(CT):
                        i = pe.transpose(side[:, c, a * P:(a + 1) * P], zn[:, a, c * P:(c + 1) * P], ident[:, :])
                i.then_inc(x2T_done, 1)

            def turn_out(f):
                turn_back(oT, (oT_copied, CT * (f + 1)), oT_turned)

            def tile(i, t, w_at, width, m, chunks, hi, lo):
                for k, last in chunks:
                    w = W[:, w_at + k * width + m * P:w_at + k * width + (m + 1) * P]
                    pe.matmul(bank_of(t)[:, :], w, hi[:, k, :], start=(k == 0), stop=False)
                    mm = pe.matmul(bank_of(t)[:, :], w, lo[:, k, :], start=False, stop=last)
                    if last:
                        mm.then_inc(tile_done, 1)

            def wide(i, t0, w_at, width, ms, hi, lo, done_before):
                for k in range(HT):
                    if done_before is not None:
                        pe.wait_ge(h_lo_done, done_before + k + 1)
                    for m in ms:
                        if k == 0:
                            wait_bank(pe, i, t0 + m)
                        tile(i, t0 + m, w_at, width, m, [(k, k == HT - 1)], hi, lo)

            def first():
                spread_sums(0)
                project_y(0)
                turn_z(0)
                turn_x1(0)

            def step(i, u, ahead, behind):
                pe.wait_ge(x2_lo_done, i + 1)
                for n in range(HT):
                    for a, w_at in ((0, W1_AT), (1, W2_AT)):
                        wait_bank(pe, i, 2 * n + a)
                        tile(i, 2 * n + a, w_at, HIDDEN, n, [(0, False), (1, True)], x2_hi, x2_lo)
                    if n == 2 and behind:
                        turn_out(i - 1)
                t = i + 1
                if ahead:
                    if behind:
                        pe.wait_ge(o_norm, TILES * i)
                    spread_sums(t)
                wide(i, L2_AT, H1_AT, HIDDEN, (0, 1, 2), h_hi[0], h_lo[0], 3 * HT * i)
                if ahead:
                    project_y(t)
                wide(i, L2_AT, H1_AT, HIDDEN, (3, 4, 5), h_hi[0], h_lo[0], None)
                if ahead:
                    turn_z(t)
                wide(i, L2_AT, H1_AT, HIDDEN, (6, 7), h_hi[0], h_lo[0], None)
                wide(i, L3_AT, H2_AT, HIDDEN, (0, 1, 2), h_hi[1], h_lo[1], 3 * HT * i + HT)
                wide(i, L3_AT, H2_AT, HIDDEN, (3, 4, 5), h_hi[1], h_lo[1], None)
                if ahead:
                    turn_x1(t)
                wide(i, L3_AT, H2_AT, HIDDEN, (6, 7), h_hi[1], h_lo[1], None)
                wide(i, OUT_AT, W3_AT, DIM, (0, 1), h_hi[0], h_lo[0], 3 * HT * i + 2 * HT)

            def end():
                turn_out(BLOCKS - 1)

            blocks(pe, first, step, end)

        @block.scalar
        def _(act):
            def ln_std(n):
                act.wait_ge(ln_var_done, TILES * (n + 1))
                act.activation(std[:, :], mean_var[:, :, 1], ACT.Sqrt, bias=eps[:, :]).then_inc(ln_std_done, 1)

            def high_of_y(t):
                act.wait_ge(y_done, t + 1)
                act.wait_ge(proj_done, t)
                act.activation(y_hi[:, :, :], y[:, :, :], ACT.Copy).then_inc(y_hi_done, 1)

            def copy_z(t):
                act.wait_ge(proj_done, t + 1)
                act.wait_ge(y_lo_done, t + 1)
                for m in range(CT):
                    s = 3 * CT + m
                    i = act.activation(z[:, m, :], side[:, m, :], ACT.Identity, bias=bias[:, s:s + 1],
                                       scale=alpha[:, s:s + 1])
                i.then_inc(z_copied, 1)

            def high_of_x1(t):
                act.wait_ge(x2T_done, t + 1)
                act.activation(x2_hi[:, :, :], side[:, :, :], ACT.Copy).then_inc(x2_hi_done, 1)

            def first():
                high_of_y(0)
                copy_z(0)
                ln_std(ln_z(0))
                ln_std(ln_x1(0))
                high_of_x1(0)

            def high_of_hidden(i, n):
                act.wait_ge(prod_done, HT * i + n + 1)
                act.activation(h_hi[0][:, n, :], hid[n % 3][:, :], ACT.Copy).then_inc(hi1_done, 1)

            def gelu(i, layer, n):
                t = (L2_AT if layer == 0 else L3_AT) + n
                s = (SH1_AT if layer == 0 else SH2_AT) + n
                act.wait_ge(tile_done, NT * i + t + 1)
                done = 3 * HT * i + HT * (layer + 1) + n
                act.wait_ge(h_lo_done, done - 2)
                act.activation(hid[n % 3][:, :], bank_of(t)[:, :], ACT.Gelu,
                               scale=scales[:, s:s + 1]).then_inc(gelu_done, 1)

            def step(i, u, ahead, behind):
                t = i + 1
                for n in range(HT):
                    act.wait_ge(tile_done, NT * i + 2 * n + 1)
                    if n >= 3:
                        act.wait_ge(prod_done, HT * i + n - 2)
                    else:
                        act.wait_ge(prod_done, HT * i)
                    act.activation(gate[n % 3][:, :], bank_of(2 * n)[:, :], ACT.Silu,
                                   scale=scales[:, S1_AT + n:S1_AT + n + 1]).then_inc(gate_done, 1)
                    if n:
                        high_of_hidden(i, n - 1)
                    if n == 5 and behind:
                        ln_std(ln_out(i - 1))
                high_of_hidden(i, HT - 1)
                if ahead:
                    high_of_y(t)
                for n in range(HT):
                    gelu(i, 0, n)
                    if n == 2 and ahead:
                        copy_z(t)
                if ahead:
                    ln_std(ln_z(t))
                    ln_std(ln_x1(t))
                for n in range(HT):
                    gelu(i, 1, n)
                    if n == 5 and ahead:
                        high_of_x1(t)
                act.wait_ge(oT_turned, i)
                for m in range(CT):
                    act.wait_ge(tile_done, NT * i + OUT_AT + m + 1)
                    act.activation(oT[:, m, :], bank_of(OUT_AT + m)[:, :], ACT.Copy,
                                   scale=scales[:, S3_AT + m:S3_AT + m + 1]).then_inc(oT_copied, 1)

            def end():
                ln_std(ln_out(BLOCKS - 1))

            blocks(act, first, step, end)

        @block.vector
        def _(dve):
            def ln_stats(n, src):
                for a in range(TILES):
                    dve.bn_stats(stats[:, a, :], src[:, a, :]).then_inc(ln_stats_done, 1)
                dve.wait_ge(ln_stats_done, TILES * (n + 1))
                dve.sem_inc(ln_stats_seen, 1)
                for a in range(TILES):
                    dve.bn_aggr(mean_var[:, a, :], stats[:, a, :]).then_inc(ln_var_done, 1)

            def ln_norm(n, dst, src, done):
                dve.wait_ge(ln_std_done, n + 1)
                dve.reciprocal(rstd[:, :], std[:, :]).then_inc(ln_rstd_done, 1)
                dve.wait_ge(ln_rstd_done, n + 1)
                for a in range(TILES):
                    dve.tensor_scalar(dst[:, a, :], src[:, a, :], mean_var[:, a, 0:1], rstd[:, a:a + 1],
                                      ALU.subtract, ALU.mult).then_inc(done, 1)

            def inverse_sums(t):
                dve.wait_ge(tail_loaded, 16 * 4 * (t + 1))
                dve.wait_ge(spread_done, t)
                dve.reciprocal(rsum[:, :], sums[:, :]).then_inc(rsum_done, 1)

            def divide_y(t):
                dve.wait_ge(spread_done, t + 1)
                dve.tensor_tensor(y[:, :, :], side[:, :, :], y[:, :, :], ALU.mult).then_inc(y_done, 1)
                dve.wait_ge(y_hi_done, t + 1)
                dve.wait_ge(y_done, t + 1)
                dve.tensor_tensor(y_lo[:, :, :], y[:, :, :], y_hi[:, :, :].bitcast(F32),
                                  ALU.subtract).then_inc(y_lo_done, 1)

            def residual(t, u):
                dve.wait_ge(zT_done, t + 1)
                ln_stats(ln_z(t), side_t)
                dve.wait_ge(x2T_done, t)
                if not isinstance(t, int) or t >= 2:
                    dve.wait_ge(o_stored, 16 * (t - 1))
                ln_norm(ln_z(t), zn, side_t, zn_done)
                dve.wait_ge(zn_done, TILES * (t + 1))
                dve.tensor_tensor(x1[u][:, :, :], x1[u][:, :, :], zn[:, :, :], ALU.add).then_inc(x1_done, 1)
                dve.wait_ge(x1_done, t + 1)
                ln_stats(ln_x1(t), x1[u])
                ln_norm(ln_x1(t), zn, x1[u], x1n_done)

            def low_of_x1(t):
                dve.wait_ge(x2_hi_done, t + 1)
                dve.tensor_tensor(x2_lo[:, :, :], side[:, :, :], x2_hi[:, :, :].bitcast(F32),
                                  ALU.subtract).then_inc(x2_lo_done, 1)

            def out_stats(f):
                dve.wait_ge(oT_turned, f + 1)
                ln_stats(ln_out(f), side_t)

            def out_sum(f, u):
                ln_norm(ln_out(f), o_sb, side_t, o_norm)
                dve.wait_ge(o_norm, TILES * (f + 1))
                dve.tensor_tensor(o_sb[:, :, :], o_sb[:, :, :], x1[u][:, :, :], ALU.add).then_inc(o_done, 1)

            def first():
                inverse_sums(0)
                divide_y(0)
                residual(0, 0)
                low_of_x1(0)

            def low_of_hidden(i, layer, n):
                a = 0 if layer != 1 else 1
                if layer == 0:
                    dve.wait_ge(hi1_done, HT * i + n + 1)
                else:
                    dve.wait_ge(hi2_done, 2 * HT * i + HT * (layer - 1) + n + 1)
                dve.tensor_tensor(h_lo[a][:, n, :], hid[n % 3][:, :], h_hi[a][:, n, :].bitcast(F32),
                                  ALU.subtract).then_inc(h_lo_done, 1)

            def high_of_hidden(i, layer, n):
                a = 0 if layer != 1 else 1
                dve.wait_ge(gelu_done, 2 * HT * i + HT * (layer - 1) + n + 1)
                dve.tensor_copy(h_hi[a][:, n, :], hid[n % 3][:, :]).then_inc(hi2_done, 1)

            def step(i, u, ahead, behind):
                t = i + 1
                for n in range(HT):
                    dve.wait_ge(gate_done, HT * i + n + 1)
                    dve.wait_ge(tile_done, NT * i + 2 * n + 2)
                    dve.wait_ge(h_lo_done, 3 * HT * i + n - 2 if n > 2 else 3 * HT * i)
                    dve.scalar_tensor_tensor(hid[n % 3][:, :], bank_of(2 * n + 1)[:, :],
                                             scales[:, S2_AT + n:S2_AT + n + 1], gate[n % 3][:, :],
                                             ALU.mult, ALU.mult).then_inc(prod_done, 1)
                    if n:
                        low_of_hidden(i, 0, n - 1)
                    if n == 4 and behind:
                        out_stats(i - 1)
                    if n == 6 and behind:
                        out_sum(i - 1, 1 - u)
                low_of_hidden(i, 0, HT - 1)
                if ahead:
                    inverse_sums(t)
                    divide_y(t)
                for layer in (1, 2):
                    for n in range(HT):
                        high_of_hidden(i, layer, n)
                        if n:
                            low_of_hidden(i, layer, n - 1)
                        if n == 6 and layer == 2 and ahead:
                            low_of_x1(t)
                    low_of_hidden(i, layer, HT - 1)
                    if layer == 1 and ahead:
                        residual(t, 1 - u)

            def end():
                out_stats(BLOCKS - 1)
                dve.wait_ge(o_stored, 16 * (BLOCKS - 1))
                out_sum(BLOCKS - 1, (BLOCKS - 1) % 2)

            blocks(dve, first, step, end)


def kernel(L0_attn_x, L0_attn_Wq, L0_attn_bq, L0_attn_Wk, L0_attn_bk, L0_attn_Wv, L0_attn_bv, L0_attn_Wp,
           L0_attn_bp, L0_ffn_w1_w, L0_ffn_w1_s, L0_ffn_w2_w, L0_ffn_w2_s, L0_ffn_h1_w, L0_ffn_h1_s,
           L0_ffn_h2_w, L0_ffn_h2_s, L0_ffn_w3_w, L0_ffn_w3_s):
    import numpy as np
    import concourse.bacc as bacc
    from concourse.bass_utils import run_bass_kernel_spmd

    def rows(a):
        return a.reshape(-1, P, a.shape[-1]).transpose(1, 0, 2)

    attn = [np.asarray(a) for a in (L0_attn_Wq, L0_attn_Wk, L0_attn_Wv, L0_attn_Wp)]
    attn_b = [np.asarray(a) for a in (L0_attn_bq, L0_attn_bk, L0_attn_bv, L0_attn_bp)]
    ffn = [np.asarray(a) for a in (L0_ffn_w1_w, L0_ffn_w2_w, L0_ffn_h1_w, L0_ffn_h2_w, L0_ffn_w3_w)]
    ffn_s = [np.asarray(a) for a in (L0_ffn_w1_s, L0_ffn_w2_s, L0_ffn_h1_s, L0_ffn_h2_s, L0_ffn_w3_s)]
    arrays = {
        "x": np.asarray(L0_attn_x),
        "attn_w": rows(np.concatenate(attn)),
        "attn_wT": np.stack([rows(a.T) for a in attn], axis=1),
        "attn_b": np.concatenate(attn_b).reshape(-1, P).T,
        "ffn_w": np.concatenate([rows(a.T).reshape(P, -1) for a in ffn], axis=1),
        "ffn_s": np.concatenate(ffn_s).reshape(-1, P).T,
    }
    arrays = {name: np.ascontiguousarray(a) for name, a in arrays.items()}
    nc = bacc.Bacc("TRN2", target_bir_lowering=False, num_devices=1)
    ins = {name: nc.dram_tensor(name, a.shape, mybir.dt.from_np(a.dtype), kind="ExternalInput").ap()
           for name, a in arrays.items()}
    out = nc.dram_tensor("out", (BATCH, SEQ, DIM), F32, kind="ExternalOutput").ap()
    layer(nc, out=out, **ins)
    r = run_bass_kernel_spmd(nc, [arrays], core_ids=[0])
    return r.results[0]["out"]
```

```python
from contextlib import ExitStack
from dataclasses import dataclass

import concourse.bass as bass
from concourse import mybir

F32 = mybir.dt.float32
F32R = mybir.dt.float32r
BF16 = mybir.dt.bfloat16
I32 = mybir.dt.int32
ACT = mybir.ActivationFunctionType
ALU = mybir.AluOpType
AX = mybir.AxisListType

P = 128
BATCH, SEQ, DIM = 4, 1024, 256
HEADS, HEAD_DIM = 16, 16
HIDDEN = 1024
TOKENS = BATCH * SEQ
BLK = 512
BLOCKS = TOKENS // BLK
TILES = BLK // P
CT = DIM // P
HT = HIDDEN // P
QUAD = 4
QUADS = BATCH * HEADS // QUAD
ST = SEQ // P
QROWS = QUAD * HEAD_DIM
STACK = 6 * HEAD_DIM
STACK_M = STACK + 3
EPS = 1e-5
SCALE = HEAD_DIM ** -0.5
HEADROOM, BOUND_LIMIT = 40, 60
NORMS_LIMIT = (BOUND_LIMIT / SCALE) ** 2
NORMS_MARGIN = 1.05
LOW_BITS = 0xFFF
Q_PART = [0, 0, 1, 1, 0, 2]
K_PART = [0, 1, 0, 1, 2, 0]
W1_AT, W2_AT = 0, CT * HIDDEN
H1_AT = 2 * CT * HIDDEN
H2_AT = H1_AT + HT * HIDDEN
W3_AT = H2_AT + HT * HIDDEN
W_ALL = W3_AT + HT * DIM
W_CHUNK = W_ALL // QUADS
S1_AT, S2_AT, SH1_AT, SH2_AT, S3_AT, S_ALL = 0, HT, 2 * HT, 3 * HT, 4 * HT, 4 * HT + CT


@dataclass
class Constants:
    signs: object
    alpha: object
    bias: object
    scales: object
    ident: object
    spread: object
    gather: object
    eps: object
    top_norms: object
    wide_range: object


def layer(nc, x, attn_w, attn_wT, attn_b, ffn_w, ffn_s, out):
    dram = {}

    def scratch(name, shape, dt):
        dram[name] = nc.dram_tensor(name, shape, dt, kind="Internal").ap()
        return dram[name]

    q_scr = scratch("q_scr", (3, BATCH * DIM, SEQ), BF16)
    k_scr = scratch("k_scr", (3, BATCH * DIM, SEQ), BF16)
    v_scr = scratch("v_scr", (QUADS * P, ST, P), F32)
    m_scr = scratch("m_scr", (3, BATCH * HEADS, SEQ), BF16)
    y_scr = scratch("y_scr", (QUADS * P, SEQ), F32)
    w_scr = scratch("w_scr", (P, W_ALL), F32)

    with ExitStack() as keep:
        def sb(name, shape, dt):
            return keep.enter_context(nc.sbuf_tensor(name, shape, dt))

        c = Constants(
            signs=sb("signs", [P, 4, CT, DIM], F32R),
            alpha=sb("alpha", [P, 4 * CT], F32),
            bias=sb("bias", [P, 4 * CT], F32),
            scales=sb("scales", [P, S_ALL], F32),
            ident=sb("ident", [P, P], F32),
            spread=sb("spread", [HEADS, CT, P], F32),
            gather=sb("gather", [P, 2 * CT, 2 * HEADS], BF16),
            eps=sb("eps", [P, 1], F32),
            top_norms=sb("top_norms", [2 * HEADS, BLOCKS], F32),
            wide_range=sb("wide_range", [1, 1], I32),
        )
        project(nc, x, attn_w, attn_wT, attn_b, ffn_s, c, q_scr, k_scr, v_scr)
        bound_scores(nc, c, m_scr)
        row_maxima(nc, c, q_scr, k_scr, m_scr)
        W = sb("W", [P, W_ALL], F32R)
        w_bits = sb("w_bits", [P, QUADS], F32)
        attention(nc, q_scr, k_scr, v_scr, m_scr, y_scr, ffn_w, w_scr, W, w_bits)
        tail_ffn(nc, x, y_scr, c, W, w_bits, out)


def project(nc, x, attn_w, attn_wT, attn_b, ffn_s, const, q_scr, k_scr, v_scr):
    signs, alpha, bias, ident, eps, gather = (const.signs, const.alpha, const.bias, const.ident, const.eps,
                                              const.gather)
    QK = 2 * CT
    x_blk = x.rearrange("b (h t p) c -> (b h) p t c", p=P, t=TILES)
    q_rows = q_scr.rearrange("s (b c p) t -> s b p c t", p=P, c=CT)
    k_rows = k_scr.rearrange("s (b c p) t -> s b p c t", p=P, c=CT)
    v_rows = v_scr.rearrange("(b q p) s n -> b q p s n", p=P, q=HEADS // QUAD)
    with ExitStack() as ctx:
        def sb(name, shape, dt):
            return ctx.enter_context(nc.sbuf_tensor(name, shape, dt))

        def sem(name):
            return ctx.enter_context(nc.semaphore(name))

        x_in = [sb(f"x_in{u}", [P, TILES, DIM], F32) for u in range(2)]
        x_norm = [sb(f"x_norm{u}", [P, TILES, DIM], F32) for u in range(2)]
        x_hi = [sb(f"x_hi{u}", [P, CT, BLK], F32R) for u in range(2)]
        x_lo = [sb(f"x_lo{u}", [P, CT, BLK], F32R) for u in range(2)]
        qkv = sb("qkv", [P, 3 * CT, BLK], F32)
        rest = sb("rest", [P, QK, BLK], F32)
        part = [[sb(f"part{s}{u}", [P, QK, BLK], BF16) for u in range(2)] for s in range(3)]
        square = sb("square", [P, QK, BLK], BF16)
        w_nat = sb("w_nat", [P, 4 * CT, DIM], F32)
        w_tr = sb("w_tr", [P, 4, CT, DIM], F32)
        abs_sum = sb("abs_sum", [P, 4 * CT], F32)
        v_aug = [sb(f"v_aug{u}", [P, TILES, HEADS, 2 * HEAD_DIM], F32) for u in range(2)]
        stats = sb("stats", [P, TILES, 6], F32)
        mean_var = sb("mean_var", [P, TILES, 2], F32)
        std = sb("std", [P, TILES], F32)
        rstd = sb("rstd", [P, TILES], F32)
        xT_ps = ctx.enter_context(nc.psum_tensor("xT_ps", [P, CT, BLK], F32))
        qkv_ps = ctx.enter_context(nc.psum_tensor("qkv_ps", [P, 3 * CT, BLK], F32))
        norm_ps = qkv_ps[0:2 * HEADS, 2, :]
        vT_ps = qkv_ps[:, 0:2, :].rearrange("p a (t c) -> p (a t) c", c=DIM)

        x_loaded = [sem(f"x_loaded{u}") for u in range(2)]
        stats_done = sem("stats_done")
        stats_seen = sem("stats_seen")
        var_done = sem("var_done")
        std_done = sem("std_done")
        rstd_done = sem("rstd_done")
        norm_done = sem("norm_done")
        xT_done = sem("xT_done")
        hi_done = sem("hi_done")
        lo_done = sem("lo_done")
        qkv_done = sem("qkv_done")
        qk_copied = sem("qk_copied")
        v_copied = sem("v_copied")
        vT_done = sem("vT_done")
        aug_done = sem("aug_done")
        high_done = sem("high_done")
        rest_done = sem("rest_done")
        mid_done = sem("mid_done")
        low_done = sem("low_done")
        aug_set = sem("aug_set")
        square_done = sem("square_done")
        norms_done = sem("norms_done")
        norms_read = sem("norms_read")
        tr_loaded = sem("tr_loaded")
        nat_loaded = sem("nat_loaded")
        small_loaded = sem("small_loaded")
        signs_done = sem("signs_done")
        summed = sem("summed")
        alpha_done = sem("alpha_done")
        eps_set = sem("eps_set")
        filled = sem("filled")
        stored = [sem(f"stored{u}") for u in range(2)]
        STORES = 3 * 2 + HEADS // QUAD
        MT = 3 * CT

        block = ctx.enter_context(nc.Block())


        def blocks(eng, first, body):
            first(0, 0, 0)
            with eng.Fori(0, BATCH - 1) as b:
                body((b, 0, 2 * b), (b, 1, 2 * b + 1))
                body((b, 1, 2 * b + 1), (b + 1, 0, 2 * b + 2))
            b = BATCH - 1
            body((b, 0, 2 * b), (b, 1, 2 * b + 1))
            body((b, 1, 2 * b + 1), None)

        @block.sync
        def _(sp):
            def load(n, u):
                sp.dma_start(x_in[u][:, :, :], x_blk[n]).then_inc(x_loaded[u], 16)

            def first(b, u, n):
                load(0, 0)
                sp.dma_start(w_tr[:, :, :, :], attn_wT).then_inc(tr_loaded, 16)
                sp.dma_start(w_nat[:, :, :], attn_w).then_inc(nat_loaded, 16)
                sp.dma_start(bias[:, :], attn_b).then_inc(small_loaded, 16)
                load(1, 1)
                sp.dma_start(const.scales[:, :], ffn_s).then_inc(small_loaded, 16)

            def body(b, last):
                for u in range(2):
                    n = 2 * b + u
                    t0 = u * BLK
                    if not last:
                        sp.wait_ge(norm_done, TILES * (n + 1))
                        load(n + 2, u)
                    for s, (done, credit) in enumerate(((high_done, 0), (mid_done, 0), (low_done, 1))):
                        sp.wait_ge(done, credit + n + 1)
                        for scr, m in ((q_rows, 0), (k_rows, CT)):
                            sp.dma_start(scr[s, b, :, :, t0:t0 + BLK],
                                         part[s][u][:, m:m + CT, :]).then_inc(stored[u], 16)
                    sp.wait_ge(aug_done, n + 1)
                    for q in range(HEADS // QUAD):
                        sp.dma_start(v_rows[b, q, :, TILES * u:TILES * (u + 1), :],
                                     v_aug[u][:, :, QUAD * q:QUAD * (q + 1), :]
                                     .rearrange("p t h n -> p t (h n)")).then_inc(stored[u], 16)

            first(0, 0, 0)
            with sp.Fori(0, BATCH - 1) as b:
                body(b, False)
            body(BATCH - 1, True)
            for u in range(2):
                sp.wait_ge(stored[u], 16 * (STORES * BATCH + 1))

        @block.vector
        def _(dve):
            def normalise(b, u, n):
                dve.wait_ge(x_loaded[u], 16 * (b + 1))
                for t in range(TILES):
                    dve.bn_stats(stats[:, t, :], x_in[u][:, t, :]).then_inc(stats_done, 1)
                dve.wait_ge(stats_done, TILES * (n + 1))
                dve.sem_inc(stats_seen, 1)
                for t in range(TILES):
                    dve.bn_aggr(mean_var[:, t, :], stats[:, t, :]).then_inc(var_done, 1)
                dve.wait_ge(std_done, n + 1)
                dve.reciprocal(rstd[:, :], std[:, :]).then_inc(rstd_done, 1)
                dve.wait_ge(rstd_done, n + 1)
                dve.wait_ge(xT_done, n)
                for t in range(TILES):
                    dve.tensor_scalar(x_norm[u][:, t, :], x_in[u][:, t, :], mean_var[:, t, 0:1],
                                      rstd[:, t:t + 1], ALU.subtract, ALU.mult).then_inc(norm_done, 1)

            def low_of_x(b, u, n):
                dve.wait_ge(hi_done, n + 1)
                dve.tensor_tensor(x_lo[u][:, :, :], xT_ps[:, :, :], x_hi[u][:, :, :].bitcast(F32),
                                  ALU.subtract).then_inc(lo_done, 1)

            def parts(b, u, n):
                dve.wait_ge(qk_copied, QK * (n + 1))
                dve.wait_ge(stored[u], 16 * (STORES * b + 1))
                dve.tensor_copy(part[0][u][:, :, :], qkv[:, 0:QK, :]).then_inc(high_done, 1)
                dve.wait_ge(high_done, n + 1)
                dve.wait_ge(low_done, n + 1)
                dve.tensor_tensor(rest[:, :, :], qkv[:, 0:QK, :], part[0][u][:, :, :],
                                  ALU.subtract).then_inc(rest_done, 1)
                dve.wait_ge(rest_done, n + 2)
                dve.tensor_copy(part[1][u][:, :, :], rest[:, :, :]).then_inc(mid_done, 1)

            def top_norm(b, u, n):
                dve.wait_ge(norms_done, n + 2)
                dve.tensor_reduce(const.top_norms[:, bass.ds(n, 1)], norm_ps, AX.X, ALU.max)\
                    .then_inc(norms_read, 1)

            def first(b, u, n):
                dve.memset(eps[:, :], EPS).then_inc(eps_set, 1)
                normalise(b, u, n)
                dve.wait_ge(nat_loaded, 16)
                dve.tensor_reduce(abs_sum[:, :], w_nat[:, :, :], AX.X, ALU.add,
                                  apply_absolute_value=True).then_inc(summed, 1)
                dve.wait_ge(summed, 1)
                dve.tensor_scalar(alpha[:, :], abs_sum[:, :], 1.0 / DIM, None, ALU.mult).then_inc(alpha_done, 1)
                low_of_x(b, u, n)

            def body(now, ahead):
                if ahead:
                    normalise(*ahead)
                parts(*now)
                if ahead:
                    low_of_x(*ahead)
                top_norm(*now)

            blocks(dve, first, body)

        @block.gpsimd
        def _(pool):
            pool.memset(ident[:, :], 0.0).then_inc(filled, 1)
            pool.memset(const.spread[:, :, :], 1.0).then_inc(filled, 1)
            pool.memset(gather[:, :, :], 1.0).then_inc(filled, 1)
            pool.wait_ge(filled, 3)
            pool.affine_select(out=ident[:, :], in_=ident[:, :], compare_op=ALU.not_equal, fill=1.0,
                               base=0, pattern=[[-1, P]], channel_multiplier=1).then_inc(filled, 1)
            pool.affine_select(out=const.spread[:, :, :], in_=const.spread[:, :, :], compare_op=ALU.is_ge,
                               fill=0.0, base=0, pattern=[[P, CT], [1, P]],
                               channel_multiplier=-HEAD_DIM).then_inc(filled, 1)
            pool.affine_select(out=gather[:, :, :], in_=gather[:, :, :], compare_op=ALU.is_ge, fill=0.0,
                               base=0, pattern=[[P, QK], [-HEAD_DIM, 2 * HEADS]],
                               channel_multiplier=1).then_inc(filled, 1)
            pool.wait_ge(filled, 6)
            pool.affine_select(out=const.spread[:, :, :], in_=const.spread[:, :, :], compare_op=ALU.is_ge,
                               fill=0.0, base=HEAD_DIM - 1, pattern=[[-P, CT], [-1, P]],
                               channel_multiplier=HEAD_DIM).then_inc(filled, 1)
            pool.affine_select(out=gather[:, :, :], in_=gather[:, :, :], compare_op=ALU.is_ge, fill=0.0,
                               base=HEAD_DIM - 1, pattern=[[-P, QK], [HEAD_DIM, 2 * HEADS]],
                               channel_multiplier=-1).then_inc(filled, 1)
            pool.sem_inc(low_done, 1)
            pool.sem_inc(rest_done, 1)
            pool.sem_inc(vT_done, 1)
            pool.sem_inc(norms_done, 1)
            for u in range(2):
                pool.sem_inc(stored[u], 16)
            for u in range(2):
                pool.memset(v_aug[u][:, :, :, HEAD_DIM:HEAD_DIM + 1], 1.0).then_inc(aug_set, 1)
                pool.memset(v_aug[u][:, :, :, HEAD_DIM + 1:], 0.0).then_inc(aug_set, 1)
            with pool.Fori(0, BATCH) as b:
                for u in range(2):
                    n = 2 * b + u
                    pool.wait_ge(high_done, n + 1)
                    pool.wait_ge(norms_done, n + 1)
                    pool.tensor_tensor(square[:, :, :], part[0][u][:, :, :], part[0][u][:, :, :],
                                       ALU.mult).then_inc(square_done, 1)
                    pool.wait_ge(mid_done, n + 1)
                    pool.wait_ge(stored[u], 16 * (STORES * b + 1))
                    pool.tensor_tensor(part[2][u][:, :, :], rest[:, :, :], part[1][u][:, :, :],
                                       ALU.subtract).then_inc(low_done, 1)

        @block.scalar
        def _(act):
            def std_of(b, u, n):
                act.wait_ge(var_done, TILES * (n + 1))
                act.activation(std[:, :], mean_var[:, :, 1], ACT.Sqrt, bias=eps[:, :]).then_inc(std_done, 1)

            def high_of_x(b, u, n):
                act.wait_ge(xT_done, n + 1)
                act.activation(x_hi[u][:, :, :], xT_ps[:, :, :], ACT.Copy).then_inc(hi_done, 1)

            def copy_qkv(b, u, n):
                act.wait_ge(rest_done, n + 1)
                for m in range(MT):
                    act.wait_ge(qkv_done, MT * n + m + 1)
                    if m == QK:
                        act.wait_ge(vT_done, n + 1)
                    act.activation(qkv[:, m, :], qkv_ps[:, m, :], ACT.Identity, bias=bias[:, m:m + 1],
                                   scale=alpha[:, m:m + 1]).then_inc(qk_copied if m < QK else v_copied, 1)

            def copy_v(b, u, n):
                act.wait_ge(vT_done, n + 2)
                act.wait_ge(stored[u], 16 * (STORES * b + 1))
                act.activation(v_aug[u][:, :, :, 0:HEAD_DIM], vT_ps.rearrange("p t (h d) -> p t h d", d=HEAD_DIM),
                               ACT.Copy).then_inc(aug_done, 1)

            def first(b, u, n):
                act.wait_ge(eps_set, 1)
                std_of(b, u, n)
                act.wait_ge(tr_loaded, 16)
                act.activation(signs[:, :, :, :], w_tr[:, :, :, :], ACT.Sign).then_inc(signs_done, 1)
                high_of_x(b, u, n)
                act.wait_ge(alpha_done, 1)
                act.wait_ge(small_loaded, 32)
                act.wait_ge(aug_set, 4)

            def body(now, ahead):
                if ahead:
                    std_of(*ahead)
                copy_qkv(*now)
                copy_v(*now)
                if ahead:
                    high_of_x(*ahead)

            blocks(act, first, body)

        @block.tensor
        def _(pe):
            def turn_x(b, u, n):
                pe.wait_ge(norm_done, TILES * (n + 1))
                pe.wait_ge(lo_done, n)
                for t in range(TILES):
                    for c in range(CT):
                        i = pe.transpose(xT_ps[:, c, t * P:(t + 1) * P],
                                         x_norm[u][:, t, c * P:(c + 1) * P], ident[:, :])
                i.then_inc(xT_done, 1)

            def project_x(b, u, n):
                pe.wait_ge(lo_done, n + 1)
                pe.wait_ge(aug_done, n)
                for m in range(MT):
                    if m == 2:
                        pe.wait_ge(norms_read, n)
                    for c in range(CT):
                        w = signs[:, m // CT, c, (m % CT) * P:(m % CT + 1) * P]
                        pe.matmul(qkv_ps[:, m, :], w, x_hi[u][:, c, :], start=(c == 0), stop=False)
                        i = pe.matmul(qkv_ps[:, m, :], w, x_lo[u][:, c, :], start=False, stop=(c == CT - 1))
                    i.then_inc(qkv_done, 1)

            def turn_v(b, u, n):
                pe.wait_ge(qk_copied, QK * (n + 1))
                pe.wait_ge(v_copied, CT * (n + 1))
                for t in range(TILES):
                    for c in range(CT):
                        i = pe.transpose(vT_ps[:, t, c * P:(c + 1) * P],
                                         qkv[:, QK + c, t * P:(t + 1) * P], ident[:, :])
                i.then_inc(vT_done, 1)

            def sum_squares(b, u, n):
                pe.wait_ge(square_done, n + 1)
                for m in range(QK):
                    i = pe.matmul(norm_ps, gather[:, m, :], square[:, m, :], start=(m == 0), stop=(m == QK - 1))
                i.then_inc(norms_done, 1)

            def first(b, u, n):
                pe.wait_ge(filled, 8)
                turn_x(b, u, n)
                pe.wait_ge(signs_done, 1)
                project_x(b, u, n)

            def body(now, ahead):
                if ahead:
                    turn_x(*ahead)
                turn_v(*now)
                sum_squares(*now)
                if ahead:
                    project_x(*ahead)

            blocks(pe, first, body)


def bound_scores(nc, const, m_scr):
    ROWS = BATCH * HEADS
    with (nc.sbuf_tensor("top_of_blocks", [2 * HEADS, 1], F32) as top,
          nc.sbuf_tensor("top_qk", [1, 2], F32) as top_qk,
          nc.sbuf_tensor("product", [1, 1], F32) as product,
          nc.sbuf_tensor("bound", [1, 1], F32) as bound,
          nc.sbuf_tensor("ones", [1, ROWS], F32) as ones,
          nc.sbuf_tensor("zeros", [ROWS, SEQ], BF16) as zeros,
          nc.sbuf_tensor("shift", [ROWS, SEQ], BF16) as shift,
          nc.psum_tensor("top_ps", [1, 2 * HEADS], F32) as top_ps,
          nc.psum_tensor("bound_ps", [ROWS, 1], F32) as bound_ps,
          nc.semaphore("bd_set") as bd_set, nc.semaphore("bd_top") as bd_top,
          nc.semaphore("bd_turned") as bd_turned, nc.semaphore("bd_product") as bd_product,
          nc.semaphore("bd_root") as bd_root, nc.semaphore("bd_spread") as bd_spread,
          nc.semaphore("bd_shift") as bd_shift, nc.semaphore("bd_stored") as bd_stored,
          nc.Block() as block):

        @block.gpsimd
        def _(pool):
            pool.memset(ones[:, :], 1.0).then_inc(bd_set, 1)
            pool.memset(zeros[:, :], 0.0).then_inc(bd_set, 1)

        @block.vector
        def _(dve):
            dve.tensor_reduce(top[:, :], const.top_norms[:, :], AX.X, ALU.max).then_inc(bd_top, 1)
            dve.wait_ge(bd_turned, 1)
            dve.tensor_reduce(top_qk[:, :], top_ps[:, :].rearrange("a (s h) -> a s h", s=2), AX.X,
                              ALU.max).then_inc(bd_top, 1)
            dve.wait_ge(bd_top, 2)
            dve.tensor_scalar(product[:, :], top_qk[:, 0:1], top_qk[:, 1:2], NORMS_MARGIN, ALU.mult,
                              ALU.mult).then_inc(bd_product, 1)
            dve.wait_ge(bd_product, 1)
            dve.tensor_scalar(const.wide_range[:, :], product[:, :], NORMS_LIMIT, None, ALU.is_gt)
            dve.wait_ge(bd_spread, 1)
            dve.wait_ge(bd_set, 2)
            dve.tensor_scalar(shift[:, :], zeros[:, :], bound_ps[:, 0:1],
                              HEADROOM / SCALE, ALU.subtract, ALU.add).then_inc(bd_shift, 1)

        @block.scalar
        def _(act):
            act.wait_ge(bd_product, 1)
            act.activation(bound[:, :], product[:, :], ACT.Sqrt).then_inc(bd_root, 1)

        @block.tensor
        def _(pe):
            pe.wait_ge(bd_top, 1)
            pe.transpose(top_ps[:, :], top[:, :], const.ident[0:2 * HEADS, 0:2 * HEADS]).then_inc(bd_turned, 1)
            pe.wait_ge(bd_root, 1)
            pe.wait_ge(bd_set, 2)
            pe.matmul(bound_ps[:, :], ones[:, :], bound[:, :], start=True, stop=True).then_inc(bd_spread, 1)

        @block.sync
        def _(sp):
            sp.wait_ge(bd_shift, 1)
            for s, src in enumerate((shift, zeros, zeros)):
                sp.dma_start(m_scr[s], src[:, :]).then_inc(bd_stored, 16)
            sp.wait_ge(bd_stored, 48)


def row_maxima(nc, const, q_scr, k_scr, m_scr):
    rows = m_scr.rearrange("s h (i p) -> (h i) s p", p=P)
    with ExitStack() as ctx:
        def sb(name, shape, dt):
            return ctx.enter_context(nc.sbuf_tensor(name, shape, dt))

        def sem(name):
            return ctx.enter_context(nc.semaphore(name))

        q_st = sb("q_st", [STACK, QUAD, SEQ], BF16)
        k_st = sb("k_st", [STACK, QUAD, SEQ], BF16)
        top = sb("top", [P, QUAD * ST], F32)
        neg = sb("neg", [QUAD * ST, P], F32)
        left = sb("left", [QUAD * ST, P], F32)
        left2 = sb("left2", [QUAD * ST, P], F32)
        m_part = sb("m_part", [QUAD * ST, 3, P], BF16)
        s_ps = [ctx.enter_context(nc.psum_tensor(f"s_ps{i}", [P, SEQ], F32)) for i in range(3)]
        t_ps = ctx.enter_context(nc.psum_tensor("t_ps", [QUAD * ST, P], F32))
        loaded = sem("mx_loaded")
        scored = sem("mx_scored")
        reduced = sem("mx_reduced")
        turned = sem("mx_turned")
        stepped = sem("mx_stepped")
        stored = sem("mx_stored")
        block = ctx.enter_context(nc.Block())
        N = QUAD * ST

        @block.sync
        def _(sp):
            wide = sp.value_load(const.wide_range[:, :], min_val=0, max_val=1)
            with sp.If(wide):
                with sp.Fori(0, QUADS) as g:
                    sp.wait_ge(turned, g + 1)
                    for i in range(6):
                        at = slice(i * HEAD_DIM, (i + 1) * HEAD_DIM)
                        for st, scr, s in ((q_st, q_scr, Q_PART[i]), (k_st, k_scr, K_PART[i])):
                            sp.dma_start(st[at, :, :], scr[s, bass.ds(g * QROWS, QROWS), :]
                                         .rearrange("(j d) t -> d j t", d=HEAD_DIM)).then_inc(loaded, 16)
                    sp.wait_ge(stepped, 6 * (g + 1) + 1)
                    sp.dma_start(rows[bass.ds(g * N, N), :, :], m_part[:, :, :]).then_inc(stored, 16)
                sp.wait_ge(stored, 16 * (QUADS + 1))

        @block.scalar
        def _(act):
            for s in (turned, stepped, reduced):
                act.sem_inc(s, 1)
            act.sem_inc(stored, 16)

        @block.tensor
        def _(pe):
            wide = pe.value_load(const.wide_range[:, :], min_val=0, max_val=1)
            with pe.If(wide):
                with pe.Fori(0, QUADS) as g:
                    pe.wait_ge(loaded, 16 * 12 * (g + 1))
                    for a in range(N):
                        j, t = divmod(a, ST)
                        if a >= 3:
                            pe.wait_ge(reduced, g * N + a - 1)
                        else:
                            pe.wait_ge(reduced, g * N + 1)
                        for h in range(2):
                            i = pe.matmul(s_ps[a % 3][:, h * BLK:(h + 1) * BLK], q_st[:, j, t * P:(t + 1) * P],
                                          k_st[:, j, h * BLK:(h + 1) * BLK], start=True, stop=True)
                        i.then_inc(scored, 1)
                    pe.wait_ge(reduced, (g + 1) * N + 1)
                    pe.wait_ge(stepped, 6 * g + 1)
                    pe.transpose(t_ps[:, :], top[:, :], const.ident[:, :]).then_inc(turned, 1)

        @block.vector
        def _(dve):
            wide = dve.value_load(const.wide_range[:, :], min_val=0, max_val=1)
            with dve.If(wide):
                with dve.Fori(0, QUADS) as g:
                    dve.wait_ge(turned, g + 1)
                    for a in range(N):
                        dve.wait_ge(scored, g * N + a + 1)
                        dve.tensor_reduce(top[:, a:a + 1], s_ps[a % 3][:, :], AX.X, ALU.max).then_inc(reduced, 1)
                    dve.wait_ge(turned, g + 2)
                    dve.wait_ge(stored, 16 * (g + 1))
                    k = 6 * g + 1
                    dve.tensor_scalar(neg[:, :], t_ps[:, :], -1.0, None, ALU.mult).then_inc(stepped, 1)
                    dve.wait_ge(stepped, k + 1)
                    dve.tensor_copy(m_part[:, 0, :], neg[:, :]).then_inc(stepped, 1)
                    dve.wait_ge(stepped, k + 2)
                    dve.tensor_tensor(left[:, :], neg[:, :], m_part[:, 0, :], ALU.subtract).then_inc(stepped, 1)
                    dve.wait_ge(stepped, k + 3)
                    dve.tensor_copy(m_part[:, 1, :], left[:, :]).then_inc(stepped, 1)
                    dve.wait_ge(stepped, k + 4)
                    dve.tensor_tensor(left2[:, :], left[:, :], m_part[:, 1, :], ALU.subtract).then_inc(stepped, 1)
                    dve.wait_ge(stepped, k + 5)
                    dve.tensor_copy(m_part[:, 2, :], left2[:, :]).then_inc(stepped, 1)


def attention(nc, q_scr, k_scr, v_scr, m_scr, y_scr, ffn_w, w_scr, W, w_bits):
    with ExitStack() as ctx:
        def sb(name, shape, dt):
            return ctx.enter_context(nc.sbuf_tensor(name, shape, dt))

        def sem(name):
            return ctx.enter_context(nc.semaphore(name))

        q_st = [sb(f"q_st{u}", [STACK_M, QUAD, SEQ], BF16) for u in range(2)]
        k_st = [sb(f"k_st{u}", [STACK_M, QUAD, SEQ], BF16) for u in range(2)]
        v_st = [sb(f"v_st{u}", [P, ST, P], F32) for u in range(2)]
        probs = [[sb(f"probs{w}{j}", [P, SEQ], F32) for j in range(QUAD)] for w in range(2)]
        y_sb = [sb(f"y_sb{u}", [P, SEQ], F32) for u in range(2)]
        s_ps = [ctx.enter_context(nc.psum_tensor(f"sc_ps{i}", [P, SEQ], F32)) for i in range(3)]
        y_ps = ctx.enter_context(nc.psum_tensor("y_ps", [P, SEQ], F32))
        loaded = [sem(f"loaded{u}") for u in range(2)]
        ones_set = sem("ones_set")
        scored = sem("scored")
        probs_ready = sem("probs_ready")
        pv_done = sem("pv_done")
        y_copied = sem("y_copied")
        y_stored = [sem(f"y_stored{u}") for u in range(2)]
        w_in_scr = sem("w_in_scr")
        low_bits = sb("low_bits", [P, W_CHUNK], I32)
        low_bits_done = sem("low_bits_done")
        w_seen = sem("w_seen")
        w_loaded = sem("w_loaded")
        LOADS = 6 * 2 + 1 + 1
        N = QUAD * ST
        block = ctx.enter_context(nc.Block())

        @block.sync
        def _(sp):
            def load(g, u):
                for i in range(6):
                    at = slice(i * HEAD_DIM, (i + 1) * HEAD_DIM)
                    for st, scr, s in ((q_st, q_scr, Q_PART[i]), (k_st, k_scr, K_PART[i])):
                        sp.dma_start(st[u][at, :, :], scr[s, bass.ds(g * QROWS, QROWS), :]
                                     .rearrange("(j d) t -> d j t", d=HEAD_DIM)).then_inc(loaded[u], 16)
                sp.dma_start(q_st[u][STACK:STACK_M, :, :],
                             m_scr[:, bass.ds(g * QUAD, QUAD), :]).then_inc(loaded[u], 16)
                sp.dma_start(v_st[u][:, :, :], v_scr[bass.ds(g * P, P), :, :]).then_inc(loaded[u], 16)

            def body(h, last):
                for u in range(2):
                    g = 2 * h + u
                    sp.wait_ge(y_copied, g + 2)
                    sp.dma_start(y_scr[bass.ds(g * P, P), :], y_sb[u][:, :]).then_inc(y_stored[u], 16)
                    if not last:
                        load(g + 2, u)
                    sp.wait_ge(w_in_scr, 16 * (g + 1))
                    sp.sem_inc(w_seen, 1)
                    sp.dma_start(W[:, bass.ds(g * W_CHUNK, W_CHUNK)].bitcast(F32),
                                 w_scr[:, bass.ds(g * W_CHUNK, W_CHUNK)]).then_inc(w_loaded, 16)
                    if not (last and u):
                        to_scratch(g + 1)

            def to_scratch(g):
                sp.dma_start(w_scr[:, bass.ds(g * W_CHUNK, W_CHUNK)],
                             ffn_w[:, bass.ds(g * W_CHUNK, W_CHUNK)]).then_inc(w_in_scr, 16)

            load(0, 0)
            load(1, 1)
            to_scratch(0)
            with sp.Fori(0, QUADS // 2 - 1) as h:
                body(h, False)
            body(QUADS // 2 - 1, True)
            for u in range(2):
                sp.wait_ge(y_stored[u], 16 * (QUADS // 2 + 1))
            sp.wait_ge(w_loaded, 16 * QUADS)

        @block.gpsimd
        def _(pool):
            pool.sem_inc(y_copied, 1)
            for u in range(2):
                pool.sem_inc(y_stored[u], 16)
            for u in range(2):
                pool.memset(k_st[u][STACK:STACK_M, :, :], 1.0).then_inc(ones_set, 1)

        @block.tensor
        def _(pe):
            def pv(g, u, s):
                pe.wait_ge(probs_ready, 3 + g * N + QUAD * (s + 1))
                for tb in range(2):
                    for j in range(QUAD):
                        i = pe.matmul(y_ps[32 * j:32 * (j + 1), tb * BLK:(tb + 1) * BLK],
                                      v_st[u][:, s, 32 * j:32 * (j + 1)],
                                      probs[s % 2][j][:, tb * BLK:(tb + 1) * BLK],
                                      start=(s == 0), stop=(s == ST - 1), tile_position=(0, 32 * j))
                i.then_inc(pv_done, 1)

            pe.wait_ge(ones_set, 2)
            with pe.Fori(0, QUADS // 2) as h:
                for u in range(2):
                    g = 2 * h + u
                    pe.wait_ge(loaded[u], 16 * LOADS * (h + 1))
                    for s in range(ST):
                        for j in range(QUAD):
                            a = s * QUAD + j
                            pe.wait_ge(probs_ready, g * N + ((2, 3, 1)[a] if a < 3 else a + 1))
                            for tb in range(2):
                                i = pe.matmul(s_ps[a % 3][:, tb * BLK:(tb + 1) * BLK],
                                              k_st[u][:, j, s * P:(s + 1) * P],
                                              q_st[u][:, j, tb * BLK:(tb + 1) * BLK], start=True, stop=True)
                            i.then_inc(scored, 1)
                        if s == 1:
                            pe.wait_ge(y_copied, g + 1)
                        if s >= 1:
                            pv(g, u, s - 1)
                    pv(g, u, ST - 1)

        @block.scalar
        def _(act):
            act.sem_inc(pv_done, 2)
            act.sem_inc(probs_ready, 3)
            with act.Fori(0, QUADS // 2) as h:
                for u in range(2):
                    g = 2 * h + u
                    for s in range(ST):
                        act.wait_ge(pv_done, g * ST + s + 1)
                        for j in range(QUAD):
                            a = s * QUAD + j
                            act.wait_ge(scored, g * N + a + 1)
                            act.activation(probs[s % 2][j][:, :], s_ps[a % 3][:, :], ACT.Exp,
                                           scale=SCALE).then_inc(probs_ready, 1)

        @block.vector
        def _(dve):
            with dve.Fori(0, QUADS // 2) as h:
                for u in range(2):
                    g = 2 * h + u
                    dve.wait_ge(pv_done, 2 + (g + 1) * ST)
                    dve.wait_ge(y_stored[u], 16 * (h + 1))
                    dve.tensor_copy(y_sb[u][:, :], y_ps[:, :]).then_inc(y_copied, 1)
                    dve.wait_ge(w_loaded, 16 * (g + 1))
                    dve.tensor_scalar(low_bits[:, :], W[:, bass.ds(g * W_CHUNK, W_CHUNK)].bitcast(I32), LOW_BITS,
                                      None, ALU.bitwise_and).then_inc(low_bits_done, 1)
                    dve.wait_ge(low_bits_done, g + 1)
                    dve.tensor_reduce(w_bits[:, bass.ds(g, 1)], low_bits[:, :], AX.X, ALU.max)


def tail_ffn(nc, x, y_scr, const, W, w_bits, out):
    signs, alpha, bias, scales, ident, spread, eps = (const.signs, const.alpha, const.bias, const.scales,
                                                      const.ident, const.spread, const.eps)
    x_blk = x.rearrange("b (h t p) c -> (b h) p t c", p=P, t=TILES)
    o_blk = out.rearrange("b (h t p) c -> (b h) p t c", p=P, t=TILES)
    y_blk = y_scr.rearrange("(b c a d) t -> b c a d t", b=BATCH, c=CT, d=2 * HEAD_DIM)
    y_heads = y_scr.rearrange("(b h d) t -> b h d t", b=BATCH, d=2 * HEAD_DIM)
    with ExitStack() as ctx:
        def sb(name, shape, dt):
            return ctx.enter_context(nc.sbuf_tensor(name, shape, dt))

        def sem(name):
            return ctx.enter_context(nc.semaphore(name))

        y = sb("y", [P, CT, BLK], F32)
        sums = sb("sums", [HEADS, BLK], F32)
        rsum = sb("rsum", [HEADS, BLK], F32)
        zn = sb("zn", [P, TILES, DIM], F32)
        x1 = [sb(f"x1_{u}", [P, TILES, DIM], F32) for u in range(2)]
        x2_hi = sb("x2_hi", [P, CT, BLK], F32R)
        x2_lo = sb("x2_lo", [P, CT, BLK], F32R)
        y_hi, y_lo = x2_hi, x2_lo
        z = y
        h_hi = [sb(f"h_hi{a}", [P, HT, BLK], F32R) for a in range(2)]
        h_lo = [sb(f"h_lo{a}", [P, HT, BLK], F32R) for a in range(2)]
        gate = [sb(f"gate{a}", [P, BLK], F32) for a in range(3)]
        hid = [sb(f"hid{a}", [P, BLK], F32) for a in range(3)]
        oT = sb("oT", [P, CT, BLK], F32)
        o_sb = zn
        stats = sb("ln_stats", [P, TILES, 6], F32)
        mean_var = sb("ln_mean_var", [P, TILES, 2], F32)
        std = sb("ln_std", [P, TILES], F32)
        rstd = sb("ln_rstd", [P, TILES], F32)
        BANKS = 6
        bank = [ctx.enter_context(nc.psum_tensor(f"ffn_ps{a}", [P, BLK], F32)) for a in range(BANKS)]
        side = ctx.enter_context(nc.psum_tensor("side_ps", [P, CT, BLK], F32))
        side_t = side[:, :, :].rearrange("p a (t c) -> p (a t) c", c=DIM)

        top_row_bits = sb("top_row_bits", [P, 1], F32)
        any_low = sb("any_low", [1, 1], I32)
        top_bits = sb("top_bits", [1, 1], F32)
        y_loaded = sem("y_loaded")
        x_loaded = [sem(f"xr_loaded{u}") for u in range(2)]
        bits_done = sem("bits_done")
        bits_turned = sem("bits_turned")
        rsum_done = sem("rsum_done")
        spread_done = sem("spread_done")
        y_done = sem("y_done")
        y_hi_done = sem("y_hi_done")
        y_lo_done = sem("y_lo_done")
        proj_done = sem("proj_done")
        z_copied = sem("z_copied")
        zT_done = sem("zT_done")
        zn_done = sem("zn_done")
        x1_done = sem("x1_done")
        x1n_done = sem("x1n_done")
        x2T_done = sem("x2T_done")
        x2_hi_done = sem("x2_hi_done")
        x2_lo_done = sem("x2_lo_done")
        ln_stats_done = sem("ln_stats_done")
        ln_stats_seen = sem("ln_stats_seen")
        ln_var_done = sem("ln_var_done")
        ln_std_done = sem("ln_std_done")
        ln_rstd_done = sem("ln_rstd_done")
        tile_done = sem("tile_done")
        gate_done = sem("gate_done")
        prod_done = sem("prod_done")
        hi1_done = sem("hi1_done")
        gelu_done = sem("gelu_done")
        hi2_done = sem("hi2_done")
        h_lo_done = sem("h_lo_done")
        oT_copied = sem("oT_copied")
        oT_turned = sem("oT_turned")
        o_norm = sem("o_norm")
        o_done = sem("o_done")
        o_stored = sem("o_stored")

        kinds = ["gate", "prod"] * HT + ["gelu"] * (2 * HT) + ["out"] * CT
        NT = len(kinds)
        reader = {"gate": gate_done, "prod": prod_done, "gelu": gelu_done, "out": oT_copied}
        per_block = {k: kinds.count(k) for k in reader}
        L2_AT, L3_AT, OUT_AT = 2 * HT, 3 * HT, 4 * HT

        def bank_of(t):
            return bank[t % BANKS]

        def wait_bank(pe, i, t):
            if t >= BANKS:
                before, blk = t - BANKS, i
            else:
                before, blk = max(p for p in range(NT) if p % BANKS == t), i - 1
                if isinstance(i, int) and i == 0:
                    return
            k = kinds[before]
            pe.wait_ge(reader[k], per_block[k] * blk + kinds[:before + 1].count(k))

        def ln_z(t):
            return 3 * t - 1 if not isinstance(t, int) or t else 0

        def ln_x1(t):
            return 3 * t if not isinstance(t, int) or t else 1

        def ln_out(f):
            return 3 * f + 4 if not isinstance(f, int) or f < BLOCKS - 1 else 3 * f + 2

        block = ctx.enter_context(nc.Block())

        def blocks(eng, first, step, end):
            first()
            step(0, 0, (0, 1), None)
            with eng.Fori(0, BATCH - 1) as b:
                step(2 * b + 1, 1, (b + 1, 0), (b, 0))
                step(2 * b + 2, 0, (b + 1, 1), (b, 1))
            step(BLOCKS - 1, 1, None, (BATCH - 1, 0))
            end()

        @block.sync
        def _(sp):
            def load_y(t, b, u):
                sp.wait_ge(zT_done, t)
                for c in range(CT):
                    sp.dma_start(y[:, c, :], y_blk[b, c, :, 0:HEAD_DIM, u * BLK:(u + 1) * BLK])\
                        .then_inc(y_loaded, 16)
                sp.dma_start(sums[:, :], y_heads[b, :, HEAD_DIM, u * BLK:(u + 1) * BLK]).then_inc(y_loaded, 16)

            def load_x(t, u):
                if not isinstance(t, int) or t >= 2:
                    sp.wait_ge(o_done, t - 1)
                sp.dma_start(x1[u][:, :, :], x_blk[t]).then_inc(x_loaded[u], 16)

            def store(f):
                sp.wait_ge(o_done, f + 1)
                sp.dma_start(o_blk[f], o_sb[:, :, :]).then_inc(o_stored, 16)

            def first():
                load_y(0, 0, 0)
                load_x(0, 0)

            def step(i, u, ahead, behind):
                if ahead:
                    load_y(i + 1, *ahead)
                if behind:
                    store(i - 1)
                if ahead:
                    load_x(i + 1, 1 - u)

            blocks(sp, first, step, lambda: store(BLOCKS - 1))
            sp.wait_ge(o_stored, 16 * BLOCKS)

        @block.tensor
        def _(pe):
            def spread_sums(t):
                pe.wait_ge(rsum_done, t + 1)
                pe.wait_ge(x2_lo_done, t)
                for c in range(CT):
                    i = pe.matmul(side[:, c, :], spread[:, c, :], rsum[:, :], start=True, stop=True)
                i.then_inc(spread_done, 1)

            def project_y(t):
                pe.wait_ge(y_hi_done, t + 1)
                pe.wait_ge(y_lo_done, t + 1)
                for m in range(CT):
                    for c in range(CT):
                        w = signs[:, 3, c, m * P:(m + 1) * P]
                        pe.matmul(side[:, m, :], w, y_hi[:, c, :], start=(c == 0), stop=False)
                        i = pe.matmul(side[:, m, :], w, y_lo[:, c, :], start=False, stop=(c == CT - 1))
                i.then_inc(proj_done, 1)

            def turn_back(src, copied, turned):
                pe.wait_ge(*copied)
                for t in range(TILES):
                    for c in range(CT):
                        i = pe.transpose(side_t[:, t, c * P:(c + 1) * P], src[:, c, t * P:(t + 1) * P], ident[:, :])
                i.then_inc(turned, 1)

            def turn_z(t):
                turn_back(z, (z_copied, t + 1), zT_done)

            def turn_x1(t):
                pe.wait_ge(x1n_done, TILES * (t + 1))
                for a in range(TILES):
                    for c in range(CT):
                        i = pe.transpose(side[:, c, a * P:(a + 1) * P], zn[:, a, c * P:(c + 1) * P], ident[:, :])
                i.then_inc(x2T_done, 1)

            def turn_out(f):
                turn_back(oT, (oT_copied, CT * (f + 1)), oT_turned)

            def tile(i, t, w_at, width, m, chunks, hi, lo):
                for k, last in chunks:
                    w = W[:, w_at + k * width + m * P:w_at + k * width + (m + 1) * P].bitcast(form)
                    pe.matmul(bank_of(t)[:, :], w, hi[:, k, :].bitcast(form), start=(k == 0), stop=False)
                    mm = pe.matmul(bank_of(t)[:, :], w, lo[:, k, :].bitcast(form), start=False, stop=last)
                    if last:
                        mm.then_inc(tile_done, 1)

            def wide(i, t0, w_at, width, ms, hi, lo, done_before):
                for k in range(HT):
                    if done_before is not None:
                        pe.wait_ge(h_lo_done, done_before + k + 1)
                    for m in ms:
                        if k == 0:
                            wait_bank(pe, i, t0 + m)
                        tile(i, t0 + m, w_at, width, m, [(k, k == HT - 1)], hi, lo)

            def first():
                spread_sums(0)
                project_y(0)
                turn_z(0)
                turn_x1(0)

            def step(i, u, ahead, behind):
                pe.wait_ge(x2_lo_done, i + 1)
                for n in range(HT):
                    for a, w_at in ((0, W1_AT), (1, W2_AT)):
                        wait_bank(pe, i, 2 * n + a)
                        tile(i, 2 * n + a, w_at, HIDDEN, n, [(0, False), (1, True)], x2_hi, x2_lo)
                    if n == 2 and behind:
                        turn_out(i - 1)
                t = i + 1
                if ahead:
                    if behind:
                        pe.wait_ge(o_norm, TILES * i)
                    spread_sums(t)
                wide(i, L2_AT, H1_AT, HIDDEN, (0, 1, 2), h_hi[0], h_lo[0], 3 * HT * i)
                if ahead:
                    project_y(t)
                wide(i, L2_AT, H1_AT, HIDDEN, (3, 4, 5), h_hi[0], h_lo[0], None)
                if ahead:
                    turn_z(t)
                wide(i, L2_AT, H1_AT, HIDDEN, (6, 7), h_hi[0], h_lo[0], None)
                wide(i, L3_AT, H2_AT, HIDDEN, (0, 1, 2), h_hi[1], h_lo[1], 3 * HT * i + HT)
                wide(i, L3_AT, H2_AT, HIDDEN, (3, 4, 5), h_hi[1], h_lo[1], None)
                if ahead:
                    turn_x1(t)
                wide(i, L3_AT, H2_AT, HIDDEN, (6, 7), h_hi[1], h_lo[1], None)
                wide(i, OUT_AT, W3_AT, DIM, (0, 1), h_hi[0], h_lo[0], 3 * HT * i + 2 * HT)

            def end():
                turn_out(BLOCKS - 1)

            pe.wait_ge(bits_done, 1)
            pe.transpose(side[0:1, 0, 0:P], top_row_bits[:, :], ident[:, :]).then_inc(bits_turned, 1)
            pe.wait_ge(bits_done, 3)
            inexact = pe.value_load(any_low[:, :], min_val=0, max_val=1)
            with pe.If(inexact):
                form = F32
                blocks(pe, first, step, end)
            with pe.Else():
                form = F32R
                blocks(pe, first, step, end)

        @block.scalar
        def _(act):
            def ln_std(n):
                act.wait_ge(ln_var_done, TILES * (n + 1))
                act.activation(std[:, :], mean_var[:, :, 1], ACT.Sqrt, bias=eps[:, :]).then_inc(ln_std_done, 1)

            def high_of_y(t):
                act.wait_ge(y_done, t + 1)
                act.wait_ge(proj_done, t)
                act.activation(y_hi[:, :, :], y[:, :, :], ACT.Copy).then_inc(y_hi_done, 1)

            def copy_z(t):
                act.wait_ge(proj_done, t + 1)
                act.wait_ge(y_lo_done, t + 1)
                for m in range(CT):
                    s = 3 * CT + m
                    i = act.activation(z[:, m, :], side[:, m, :], ACT.Identity, bias=bias[:, s:s + 1],
                                       scale=alpha[:, s:s + 1])
                i.then_inc(z_copied, 1)

            def high_of_x1(t):
                act.wait_ge(x2T_done, t + 1)
                act.activation(x2_hi[:, :, :], side[:, :, :], ACT.Copy).then_inc(x2_hi_done, 1)

            def first():
                high_of_y(0)
                copy_z(0)
                ln_std(ln_z(0))
                ln_std(ln_x1(0))
                high_of_x1(0)

            def high_of_hidden(i, n):
                act.wait_ge(prod_done, HT * i + n + 1)
                act.activation(h_hi[0][:, n, :], hid[n % 3][:, :], ACT.Copy).then_inc(hi1_done, 1)

            def gelu(i, layer, n):
                t = (L2_AT if layer == 0 else L3_AT) + n
                s = (SH1_AT if layer == 0 else SH2_AT) + n
                act.wait_ge(tile_done, NT * i + t + 1)
                done = 3 * HT * i + HT * (layer + 1) + n
                act.wait_ge(h_lo_done, done - 2)
                act.activation(hid[n % 3][:, :], bank_of(t)[:, :], ACT.Gelu,
                               scale=scales[:, s:s + 1]).then_inc(gelu_done, 1)

            def step(i, u, ahead, behind):
                t = i + 1
                for n in range(HT):
                    act.wait_ge(tile_done, NT * i + 2 * n + 1)
                    if n >= 3:
                        act.wait_ge(prod_done, HT * i + n - 2)
                    else:
                        act.wait_ge(prod_done, HT * i)
                    act.activation(gate[n % 3][:, :], bank_of(2 * n)[:, :], ACT.Silu,
                                   scale=scales[:, S1_AT + n:S1_AT + n + 1]).then_inc(gate_done, 1)
                    if n:
                        high_of_hidden(i, n - 1)
                    if n == 5 and behind:
                        ln_std(ln_out(i - 1))
                high_of_hidden(i, HT - 1)
                if ahead:
                    high_of_y(t)
                for n in range(HT):
                    gelu(i, 0, n)
                    if n == 2 and ahead:
                        copy_z(t)
                if ahead:
                    ln_std(ln_z(t))
                    ln_std(ln_x1(t))
                for n in range(HT):
                    gelu(i, 1, n)
                    if n == 5 and ahead:
                        high_of_x1(t)
                act.wait_ge(oT_turned, i)
                for m in range(CT):
                    act.wait_ge(tile_done, NT * i + OUT_AT + m + 1)
                    act.activation(oT[:, m, :], bank_of(OUT_AT + m)[:, :], ACT.Copy,
                                   scale=scales[:, S3_AT + m:S3_AT + m + 1]).then_inc(oT_copied, 1)

            def end():
                ln_std(ln_out(BLOCKS - 1))

            blocks(act, first, step, end)

        @block.vector
        def _(dve):
            def ln_stats(n, src):
                for a in range(TILES):
                    dve.bn_stats(stats[:, a, :], src[:, a, :]).then_inc(ln_stats_done, 1)
                dve.wait_ge(ln_stats_done, TILES * (n + 1))
                dve.sem_inc(ln_stats_seen, 1)
                for a in range(TILES):
                    dve.bn_aggr(mean_var[:, a, :], stats[:, a, :]).then_inc(ln_var_done, 1)

            def ln_norm(n, dst, src, done):
                dve.wait_ge(ln_std_done, n + 1)
                dve.reciprocal(rstd[:, :], std[:, :]).then_inc(ln_rstd_done, 1)
                dve.wait_ge(ln_rstd_done, n + 1)
                for a in range(TILES):
                    dve.tensor_scalar(dst[:, a, :], src[:, a, :], mean_var[:, a, 0:1], rstd[:, a:a + 1],
                                      ALU.subtract, ALU.mult).then_inc(done, 1)

            def inverse_sums(t):
                dve.wait_ge(y_loaded, 16 * (CT + 1) * (t + 1))
                dve.wait_ge(spread_done, t)
                dve.reciprocal(rsum[:, :], sums[:, :]).then_inc(rsum_done, 1)

            def divide_y(t):
                dve.wait_ge(spread_done, t + 1)
                dve.tensor_tensor(y[:, :, :], side[:, :, :], y[:, :, :], ALU.mult).then_inc(y_done, 1)
                dve.wait_ge(y_hi_done, t + 1)
                dve.wait_ge(y_done, t + 1)
                dve.tensor_tensor(y_lo[:, :, :], y[:, :, :], y_hi[:, :, :].bitcast(F32),
                                  ALU.subtract).then_inc(y_lo_done, 1)

            def residual(t, b, u):
                dve.wait_ge(zT_done, t + 1)
                ln_stats(ln_z(t), side_t)
                dve.wait_ge(x2T_done, t)
                if not isinstance(t, int) or t >= 2:
                    dve.wait_ge(o_stored, 16 * (t - 1))
                ln_norm(ln_z(t), zn, side_t, zn_done)
                dve.wait_ge(zn_done, TILES * (t + 1))
                dve.wait_ge(x_loaded[u], 16 * (b + 1))
                dve.tensor_tensor(x1[u][:, :, :], x1[u][:, :, :], zn[:, :, :], ALU.add).then_inc(x1_done, 1)
                dve.wait_ge(x1_done, t + 1)
                ln_stats(ln_x1(t), x1[u])
                ln_norm(ln_x1(t), zn, x1[u], x1n_done)

            def low_of_x1(t):
                dve.wait_ge(x2_hi_done, t + 1)
                dve.tensor_tensor(x2_lo[:, :, :], side[:, :, :], x2_hi[:, :, :].bitcast(F32),
                                  ALU.subtract).then_inc(x2_lo_done, 1)

            def out_stats(f):
                dve.wait_ge(oT_turned, f + 1)
                ln_stats(ln_out(f), side_t)

            def out_sum(f, u):
                ln_norm(ln_out(f), o_sb, side_t, o_norm)
                dve.wait_ge(o_norm, TILES * (f + 1))
                dve.tensor_tensor(o_sb[:, :, :], o_sb[:, :, :], x1[u][:, :, :], ALU.add).then_inc(o_done, 1)

            def first():
                inverse_sums(0)
                divide_y(0)
                residual(0, 0, 0)
                low_of_x1(0)

            def low_of_hidden(i, layer, n):
                a = 0 if layer != 1 else 1
                if layer == 0:
                    dve.wait_ge(hi1_done, HT * i + n + 1)
                else:
                    dve.wait_ge(hi2_done, 2 * HT * i + HT * (layer - 1) + n + 1)
                dve.tensor_tensor(h_lo[a][:, n, :], hid[n % 3][:, :], h_hi[a][:, n, :].bitcast(F32),
                                  ALU.subtract).then_inc(h_lo_done, 1)

            def high_of_hidden(i, layer, n):
                a = 0 if layer != 1 else 1
                dve.wait_ge(gelu_done, 2 * HT * i + HT * (layer - 1) + n + 1)
                dve.tensor_copy(h_hi[a][:, n, :], hid[n % 3][:, :]).then_inc(hi2_done, 1)

            def step(i, u, ahead, behind):
                t = i + 1
                for n in range(HT):
                    dve.wait_ge(gate_done, HT * i + n + 1)
                    dve.wait_ge(tile_done, NT * i + 2 * n + 2)
                    dve.wait_ge(h_lo_done, 3 * HT * i + n - 2 if n > 2 else 3 * HT * i)
                    dve.scalar_tensor_tensor(hid[n % 3][:, :], bank_of(2 * n + 1)[:, :],
                                             scales[:, S2_AT + n:S2_AT + n + 1], gate[n % 3][:, :],
                                             ALU.mult, ALU.mult).then_inc(prod_done, 1)
                    if n:
                        low_of_hidden(i, 0, n - 1)
                    if n == 1 and ahead:
                        inverse_sums(t)
                    if n == 4 and behind:
                        out_stats(i - 1)
                    if n == 6 and behind:
                        out_sum(i - 1, 1 - u)
                low_of_hidden(i, 0, HT - 1)
                if ahead:
                    divide_y(t)
                for layer in (1, 2):
                    for n in range(HT):
                        high_of_hidden(i, layer, n)
                        if n:
                            low_of_hidden(i, layer, n - 1)
                        if n == 6 and layer == 2 and ahead:
                            low_of_x1(t)
                    low_of_hidden(i, layer, HT - 1)
                    if layer == 1 and ahead:
                        residual(t, *ahead)

            dve.tensor_reduce(top_row_bits[:, :], w_bits[:, :], AX.X, ALU.max).then_inc(bits_done, 1)
            dve.wait_ge(bits_turned, 1)
            dve.tensor_reduce(top_bits[:, :], side[0:1, 0, 0:P], AX.X, ALU.max).then_inc(bits_done, 1)
            dve.wait_ge(bits_done, 2)
            dve.tensor_scalar(any_low[:, :], top_bits[:, :], 0.0, None, ALU.is_gt).then_inc(bits_done, 1)

            def end():
                out_stats(BLOCKS - 1)
                dve.wait_ge(o_stored, 16 * (BLOCKS - 1))
                out_sum(BLOCKS - 1, (BLOCKS - 1) % 2)

            blocks(dve, first, step, end)


def kernel(L0_attn_x, L0_attn_Wq, L0_attn_bq, L0_attn_Wk, L0_attn_bk, L0_attn_Wv, L0_attn_bv, L0_attn_Wp,
           L0_attn_bp, L0_ffn_w1_w, L0_ffn_w1_s, L0_ffn_w2_w, L0_ffn_w2_s, L0_ffn_h1_w, L0_ffn_h1_s,
           L0_ffn_h2_w, L0_ffn_h2_s, L0_ffn_w3_w, L0_ffn_w3_s):
    import numpy as np
    import concourse.bacc as bacc
    from concourse.bass_utils import run_bass_kernel_spmd

    def rows(a):
        return a.reshape(-1, P, a.shape[-1]).transpose(1, 0, 2)

    attn = [np.asarray(a) for a in (L0_attn_Wq, L0_attn_Wk, L0_attn_Wv, L0_attn_Wp)]
    attn_b = [np.asarray(a) for a in (L0_attn_bq, L0_attn_bk, L0_attn_bv, L0_attn_bp)]
    ffn = [np.asarray(a) for a in (L0_ffn_w1_w, L0_ffn_w2_w, L0_ffn_h1_w, L0_ffn_h2_w, L0_ffn_w3_w)]
    ffn_s = [np.asarray(a) for a in (L0_ffn_w1_s, L0_ffn_w2_s, L0_ffn_h1_s, L0_ffn_h2_s, L0_ffn_w3_s)]
    arrays = {
        "x": np.asarray(L0_attn_x),
        "attn_w": rows(np.concatenate(attn)),
        "attn_wT": np.stack([rows(a.T) for a in attn], axis=1),
        "attn_b": np.concatenate(attn_b).reshape(-1, P).T,
        "ffn_w": np.concatenate([rows(a.T).reshape(P, -1) for a in ffn], axis=1),
        "ffn_s": np.concatenate(ffn_s).reshape(-1, P).T,
    }
    arrays = {name: np.ascontiguousarray(a) for name, a in arrays.items()}
    nc = bacc.Bacc("TRN2", target_bir_lowering=False, num_devices=1)
    ins = {name: nc.dram_tensor(name, a.shape, mybir.dt.from_np(a.dtype), kind="ExternalInput").ap()
           for name, a in arrays.items()}
    out = nc.dram_tensor("out", (BATCH, SEQ, DIM), F32, kind="ExternalOutput").ap()
    layer(nc, out=out, **ins)
    r = run_bass_kernel_spmd(nc, [arrays], core_ids=[0])
    return r.results[0]["out"]
```

```python
from contextlib import ExitStack
from dataclasses import dataclass

import concourse.bass as bass
from concourse import mybir

F32 = mybir.dt.float32
F32R = mybir.dt.float32r
BF16 = mybir.dt.bfloat16
I32 = mybir.dt.int32
ACT = mybir.ActivationFunctionType
ALU = mybir.AluOpType
AX = mybir.AxisListType

P = 128
BATCH, SEQ, DIM = 4, 1024, 256
HEADS, HEAD_DIM = 16, 16
HIDDEN = 1024
TOKENS = BATCH * SEQ
BLK = 512
BLOCKS = TOKENS // BLK
TILES = BLK // P
CT = DIM // P
QK = 2 * CT
HT = HIDDEN // P
QUAD = 4
QUADS = BATCH * HEADS // QUAD
ST = SEQ // P
QROWS = QUAD * HEAD_DIM
STACK = 6 * HEAD_DIM
STACK_M = STACK + 3
EPS = 1e-5
SCALE = HEAD_DIM ** -0.5
HEADROOM, BOUND_LIMIT = 40, 60
NORMS_LIMIT = (BOUND_LIMIT / SCALE) ** 2
NORMS_MARGIN = 1.05
LOW_BITS = 0xFFF
Q_PART = [0, 0, 1, 1, 0, 2]
K_PART = [0, 1, 0, 1, 2, 0]
W1_AT, W2_AT = 0, CT * HIDDEN
H1_AT = 2 * CT * HIDDEN
H2_AT = H1_AT + HT * HIDDEN
W3_AT = H2_AT + HT * HIDDEN
W_ALL = W3_AT + HT * DIM
W_CHUNK = W_ALL // QUADS
S1_AT, S2_AT, SH1_AT, SH2_AT, S_ALL = 0, HT, 2 * HT, 3 * HT, 4 * HT


@dataclass
class Constants:
    signs: object
    alpha: object
    bias: object
    scales: object
    ident: object
    gather: object
    alpha_row: object
    bias_row: object
    out_row: object
    eps: object
    top_norms: object
    wide_range: object


@dataclass
class Quads:
    q: object
    k: object
    v: object
    loaded: object
    m_loaded: object
    zeros: object
    shift: object
    shift_stored: object
    stored: object


@dataclass
class TailInput:
    y: object
    sums: object
    x1: object
    y_stored: object
    y_loaded: object
    inverted: object
    y_done: object
    x_loaded: object


def x_by_block(x):
    return x.rearrange("b (h t p) c -> (b h) p t c", p=P, t=TILES)


def load_tail_y(sp, y_scr, tail_in, b, u):
    y_blk = y_scr.rearrange("(b c a d) t -> b c a d t", b=BATCH, c=CT, d=2 * HEAD_DIM)
    tokens = slice(u * BLK, (u + 1) * BLK)
    for c in range(CT):
        sp.dma_start(tail_in.y[:, c, :], y_blk[b, c, :, 0:HEAD_DIM, tokens]).then_inc(tail_in.y_loaded, 16)
        sp.dma_start(tail_in.sums[:, c, :], y_blk[b, c, :, HEAD_DIM:HEAD_DIM + 1, tokens]
                     .to_broadcast([P // HEAD_DIM, HEAD_DIM, BLK])).then_inc(tail_in.y_loaded, 16)


TAIL_LOADS = 2 * CT


INVERT_PARTS = 4


def invert_sums(dve, tail_in, t, part):
    if part == 0:
        dve.wait_ge(tail_in.y_loaded, 16 * TAIL_LOADS * (t + 1))
    n = CT * BLK // INVERT_PARTS
    sums = tail_in.sums[:, :, :].rearrange("p c t -> p (c t)")[:, part * n:(part + 1) * n]
    dve.reciprocal(sums, sums).then_inc(tail_in.inverted, 1)


def divide_y(dve, tail_in, t):
    dve.wait_ge(tail_in.inverted, INVERT_PARTS * (t + 1))
    dve.tensor_tensor(tail_in.y[:, :, :], tail_in.y[:, :, :], tail_in.sums[:, :, :], ALU.mult)\
        .then_inc(tail_in.y_done, 1)


def load_stacks(sp, q_scr, k_scr, q, k, g, done, groups=range(6)):
    for i in groups:
        at = slice(i * HEAD_DIM, (i + 1) * HEAD_DIM)
        for st, scr, s in ((q, q_scr, Q_PART[i]), (k, k_scr, K_PART[i])):
            sp.dma_start(st[at, :, :], scr[s, bass.ds(g * QROWS, QROWS), :]
                         .rearrange("(j d) t -> d j t", d=HEAD_DIM)).then_inc(done, 16)


def load_v(sp, v_scr, quads, g, u):
    sp.dma_start(quads.v[u][:, :, :], v_scr[bass.ds(g * P, P), :, :]).then_inc(quads.loaded[u], 16)


def load_quad(sp, q_scr, k_scr, v_scr, quads, g, u):
    load_stacks(sp, q_scr, k_scr, quads.q[u], quads.k[u], g, quads.loaded[u])
    load_v(sp, v_scr, quads, g, u)


QUAD_LOADS = 6 * 2 + 1
STORES = 3 * 2 + 1


def layer(nc, x, attn_w, attn_wT, attn_b, attn_b_rows, ffn_w, ffn_s, ffn_s3, out):
    dram = {}

    def scratch(name, shape, dt):
        dram[name] = nc.dram_tensor(name, shape, dt, kind="Internal").ap()
        return dram[name]

    q_scr = scratch("q_scr", (3, BATCH * DIM, SEQ), BF16)
    k_scr = scratch("k_scr", (3, BATCH * DIM, SEQ), BF16)
    v_scr = scratch("v_scr", (QUADS * P, ST, P), F32)
    m_scr = scratch("m_scr", (3, BATCH * HEADS, SEQ), BF16)
    y_scr = scratch("y_scr", (QUADS * P, SEQ), F32)
    w_scr = scratch("w_scr", (P, W_ALL), F32)

    with ExitStack() as keep, ExitStack() as until_ffn:
        def right(name, shape, dt):
            return until_ffn.enter_context(nc.sbuf_tensor(name, shape, dt, side="right"))

        def sb(name, shape, dt):
            return keep.enter_context(nc.sbuf_tensor(name, shape, dt))

        c = Constants(
            signs=sb("signs", [P, 4, CT, DIM], F32R),
            alpha=sb("alpha", [P, QK], F32),
            bias=sb("bias", [P, QK], F32),
            alpha_row=sb("alpha_row", [P, 2, DIM], F32),
            bias_row=sb("bias_row", [P, 2, DIM], F32),
            out_row=sb("out_row", [P, DIM], F32),
            scales=sb("scales", [P, S_ALL], F32),
            ident=sb("ident", [P, P], F32),
            gather=sb("gather", [P, 2 * CT, 2 * HEADS], BF16),
            eps=sb("eps", [P, 1], F32),
            top_norms=sb("top_norms", [2 * HEADS, BLOCKS], F32),
            wide_range=sb("wide_range", [1, 1], I32),
        )
        quads = Quads(
            q=[right(f"q_st{u}", [STACK_M, QUAD, SEQ], BF16) for u in range(2)],
            k=[right(f"k_st{u}", [STACK_M, QUAD, SEQ], BF16) for u in range(2)],
            v=[right(f"v_st{u}", [P, ST, P], F32) for u in range(2)],
            loaded=[keep.enter_context(nc.semaphore(f"quad_loaded{u}")) for u in range(2)],
            m_loaded=[keep.enter_context(nc.semaphore(f"m_loaded{u}")) for u in range(2)],
            zeros=right("zeros", [BATCH * HEADS, SEQ], BF16),
            shift=right("shift", [BATCH * HEADS, SEQ], BF16),
            shift_stored=keep.enter_context(nc.semaphore("shift_stored")),
            stored=[keep.enter_context(nc.semaphore(f"stored{u}")) for u in range(2)],
        )
        project(nc, x, attn_w, attn_wT, attn_b, attn_b_rows, ffn_s, ffn_s3, c, q_scr, k_scr, v_scr, m_scr, quads)
        W = sb("W", [P, W_ALL], F32R)
        w_bits = sb("w_bits", [P, QUADS], F32)
        tail_in = TailInput(
            y=sb("y", [P, CT, BLK], F32),
            sums=sb("sums", [P, CT, BLK], F32),
            x1=sb("x1_0", [P, TILES, DIM], F32),
            y_stored=[keep.enter_context(nc.semaphore(f"y_stored{u}")) for u in range(2)],
            y_loaded=keep.enter_context(nc.semaphore("y_loaded")),
            inverted=keep.enter_context(nc.semaphore("inverted")),
            y_done=keep.enter_context(nc.semaphore("y_done")),
            x_loaded=[keep.enter_context(nc.semaphore(f"xr_loaded{u}")) for u in range(2)],
        )
        attention(nc, c, q_scr, k_scr, v_scr, m_scr, y_scr, ffn_w, w_scr, W, w_bits, quads, x, tail_in)
        until_ffn.close()
        tail_ffn(nc, x, y_scr, c, W, w_bits, tail_in, out)


def project(nc, x, attn_w, attn_wT, attn_b, attn_b_rows, ffn_s, ffn_s3, const, q_scr, k_scr, v_scr, m_scr, quads):
    signs, alpha, bias, ident, eps, gather = (const.signs, const.alpha, const.bias, const.ident, const.eps,
                                              const.gather)
    ROWS = BATCH * HEADS
    x_blk = x.rearrange("b (h t p) c -> (b h) p t c", p=P, t=TILES)
    q_rows = q_scr.rearrange("s (b c p) t -> s b p c t", p=P, c=CT)
    k_rows = k_scr.rearrange("s (b c p) t -> s b p c t", p=P, c=CT)
    v_rows = v_scr.rearrange("(b q p) s n -> b q p s n", p=P, q=HEADS // QUAD)
    with ExitStack() as ctx:
        def sb(name, shape, dt):
            return ctx.enter_context(nc.sbuf_tensor(name, shape, dt))

        def sem(name):
            return ctx.enter_context(nc.semaphore(name))

        part = [[sb(f"part{s}{u}", [P, QK, BLK], BF16) for u in range(2)] for s in range(3)]
        v_aug = [sb(f"v_aug{u}", [P, HEADS // QUAD, TILES, QUAD, 2 * HEAD_DIM], F32) for u in range(2)]
        x_in = [sb(f"x_in{u}", [P, TILES, DIM], F32) for u in range(2)]
        x_norm = [sb(f"x_norm{u}", [P, TILES, DIM], F32) for u in range(2)]
        x_hi = [sb(f"x_hi{u}", [P, CT, BLK], F32R) for u in range(2)]
        x_lo = [sb(f"x_lo{u}", [P, CT, BLK], F32R) for u in range(2)]
        qk = [sb(f"qk{u}", [P, QK, BLK], F32) for u in range(2)]
        rest = [sb(f"rest{u}", [P, QK, BLK], F32) for u in range(2)]
        square = [sb(f"square{u}", [P, QK, BLK], BF16) for u in range(2)]
        top = sb("top_of_blocks", [2 * HEADS, 1], F32)
        top_qk = sb("top_qk", [1, 2], F32)
        product = sb("product", [1, 1], F32)
        warm = sb("warm", [P, 1], F32)
        bound = sb("bound", [1, 1], F32)
        ones = sb("ones", [1, ROWS], F32)
        zeros, shift, shift_stored = quads.zeros, quads.shift, quads.shift_stored
        w_nat = sb("w_nat", [P, QK, DIM], F32)
        w_tr = sb("w_tr", [P, 4, CT, DIM], F32)
        abs_sum = sb("abs_sum", [P, QK], F32)
        abs_tr = sb("abs_tr", [P, 2, CT, DIM], F32)
        mean_w = sb("mean_w", [P, P], F32)
        stats = sb("stats", [P, TILES, 6], F32)
        mean_var = sb("mean_var", [P, TILES, 2], F32)
        std = sb("std", [P, TILES], F32)
        rstd = sb("rstd", [P, TILES], F32)
        xT_ps = ctx.enter_context(nc.psum_tensor("xT_ps", [P, CT, BLK], F32))
        qk_ps = ctx.enter_context(nc.psum_tensor("qk_ps", [P, QK, BLK], F32))
        v_ps = ctx.enter_context(nc.psum_tensor("v_ps", [P, TILES, DIM], F32))
        norm_ps = xT_ps[0:2 * HEADS, 0, :]
        top_ps = xT_ps[0:1, 0, 0:2 * HEADS]
        bound_ps = xT_ps[0:ROWS, 1, 0:1]
        alpha_ps = v_ps[:, 0:2, :]

        x_loaded = [sem(f"x_loaded{u}") for u in range(2)]
        stats_done = sem("stats_done")
        stats_seen = sem("stats_seen")
        var_done = sem("var_done")
        std_done = sem("std_done")
        rstd_done = sem("rstd_done")
        norm_done = sem("norm_done")
        xT_done = sem("xT_done")
        hi_done = sem("hi_done")
        lo_done = sem("lo_done")
        qk_done = sem("qk_done")
        qk_copied = sem("qk_copied")
        v_done = sem("v_done")
        v_scaled = sem("v_scaled")
        aug_done = sem("aug_done")
        abs_done = sem("abs_done")
        alpha_summed = sem("alpha_summed")
        alpha_row_done = sem("alpha_row_done")
        high_done = sem("high_done")
        rest_done = sem("rest_done")
        mid_done = sem("mid_done")
        low_done = sem("low_done")
        aug_set = sem("aug_set")
        square_done = sem("square_done")
        norms_done = sem("norms_done")
        norms_read = sem("norms_read")
        tr_loaded = sem("tr_loaded")
        tr_v_loaded = sem("tr_v_loaded")
        mean_w_set = sem("mean_w_set")
        nat_loaded = sem("nat_loaded")
        small_loaded = sem("small_loaded")
        signs_done = sem("signs_done")
        summed = sem("summed")
        alpha_done = sem("alpha_done")
        eps_set = sem("eps_set")
        filled = sem("filled")
        ident_set = sem("ident_set")
        bound_set = sem("bound_set")
        top_done = sem("top_done")
        top_turned = sem("top_turned")
        product_done = sem("product_done")
        root_done = sem("root_done")
        bound_spread = sem("bound_spread")
        shift_done = sem("shift_done")
        stored = quads.stored

        block = ctx.enter_context(nc.Block())


        def steps(eng, first, body):
            def window(b, u):
                n = 2 * b + u
                blocks = {i: (b + (u + i) // 2, (u + i) % 2, n + i) for i in range(-2, 3)}
                if isinstance(n, int):
                    blocks = {i: k if 0 <= k[2] < BLOCKS else None for i, k in blocks.items()}
                return blocks

            first(0, 0, 0)
            body(window(0, 0))
            body(window(0, 1))
            with eng.Fori(1, BATCH - 1) as b:
                body(window(b, 0))
                body(window(b, 1))
            for n in range(BLOCKS - 2, BLOCKS + 2):
                body(window(n // 2, n % 2))

        def v_shaped(row):
            return row[:, 0, :].rearrange("p (q j d) -> p q j d", j=QUAD, d=HEAD_DIM).unsqueeze(2)\
                .to_broadcast([P, HEADS // QUAD, TILES, QUAD, HEAD_DIM])

        def is_first(n):
            return isinstance(n, int) and n == 0

        @block.sync
        def _(sp):
            def load(n, u):
                sp.dma_start(x_in[u][:, :, :], x_blk[n]).then_inc(x_loaded[u], 16)

            def store_shift():
                sp.wait_ge(shift_done, 1)
                sp.wait_ge(bound_set, 6)
                for u in range(2):
                    sp.dma_start(quads.q[u][STACK:STACK + 1, :, :],
                                 shift[u * QUAD:(u + 1) * QUAD, :]).then_inc(quads.m_loaded[u], 16)
                for s, src in enumerate((shift, zeros, zeros)):
                    sp.dma_start(m_scr[s], src[:, :]).then_inc(shift_stored, 16)

            def body(b, loads, stack_groups=None):
                for u in range(2):
                    n = 2 * b + u
                    if stack_groups:
                        if u == 0:
                            for w in range(2):
                                sp.wait_ge(stored[w], 16 * (STORES * b + 1))
                            load_v(sp, v_scr, quads, 0, 0)
                        load_stacks(sp, q_scr, k_scr, quads.q[0], quads.k[0], 0, quads.loaded[0], stack_groups[u])
                    for s, (done, credit) in enumerate(((high_done, 0), (mid_done, 0), (low_done, 1))):
                        if s == 1 and loads:
                            sp.wait_ge(norm_done, TILES * (n + 3))
                            load(n + 4, u)
                        sp.wait_ge(done, credit + n + 1)
                        for scr, m in ((q_rows, 0), (k_rows, CT)):
                            sp.dma_start(scr[s, b, :, :, u * BLK:(u + 1) * BLK],
                                         part[s][u][:, m:m + CT, :]).then_inc(stored[u], 16)
                    if isinstance(n, int) and n == BLOCKS - 1:
                        store_shift()
                    sp.wait_ge(aug_done, n + 1)
                    sp.dma_start(v_rows[b, :, :, TILES * u:TILES * (u + 1), :].rearrange("q p s n -> p q (s n)"),
                                 v_aug[u][:, :, :, :, :].rearrange("p q t j n -> p q (t j n)"))\
                        .then_inc(stored[u], 16)

            load(0, 0)
            sp.dma_start(w_tr[:, 0:2, :, :], attn_wT[:, 0:2]).then_inc(tr_loaded, 16)
            sp.dma_start(w_nat[:, :, :], attn_w).then_inc(nat_loaded, 16)
            load(1, 1)
            sp.dma_start(w_tr[:, 2:4, :, :], attn_wT[:, 2:4]).then_inc(tr_v_loaded, 16)
            sp.dma_start(bias[:, :], attn_b).then_inc(small_loaded, 16)
            for i in range(2):
                sp.dma_start(const.bias_row[:, i, :], attn_b_rows[i].partition_broadcast(P)).then_inc(small_loaded, 16)
            sp.dma_start(const.out_row[:, :], ffn_s3.partition_broadcast(P)).then_inc(small_loaded, 16)
            sp.dma_start(const.scales[:, :], ffn_s).then_inc(small_loaded, 16)
            for u in range(2):
                sp.wait_ge(norm_done, TILES * (u + 1))
                load(2 + u, u)
            with sp.Fori(0, BATCH - 2) as b:
                body(b, True)
            body(BATCH - 2, False, (range(0, 3), range(3, 6)))
            body(BATCH - 1, False)
            for u in range(2):
                sp.wait_ge(quads.m_loaded[u], 16)

        @block.vector
        def _(dve):
            def statistics(b, u, n):
                dve.wait_ge(x_loaded[u], 16 * (b + 1))
                for t in range(TILES):
                    dve.bn_stats(stats[:, t, :], x_in[u][:, t, :]).then_inc(stats_done, 1)
                dve.wait_ge(stats_done, TILES * (n + 1))
                dve.sem_inc(stats_seen, 1)
                for t in range(TILES):
                    dve.bn_aggr(mean_var[:, t, :], stats[:, t, :]).then_inc(var_done, 1)

            def normalise(b, u, n):
                dve.wait_ge(std_done, n + 1)
                dve.reciprocal(rstd[:, :], std[:, :]).then_inc(rstd_done, 1)
                dve.wait_ge(rstd_done, n + 1)
                if not isinstance(n, int) or n >= 2:
                    dve.wait_ge(xT_done, n - 1)
                for t in range(TILES):
                    dve.tensor_scalar(x_norm[u][:, t, :], x_in[u][:, t, :], mean_var[:, t, 0:1],
                                      rstd[:, t:t + 1], ALU.subtract, ALU.mult).then_inc(norm_done, 1)

            def low_of_x(b, u, n):
                dve.wait_ge(hi_done, n + 1)
                dve.tensor_tensor(x_lo[u][:, :, :], xT_ps[:, :, :], x_hi[u][:, :, :].bitcast(F32),
                                  ALU.subtract).then_inc(lo_done, 1)

            def rest_of_qk(b, u, n):
                dve.wait_ge(high_done, n + 1)
                if not is_first(n):
                    dve.wait_ge(low_done, n)
                dve.tensor_tensor(rest[u][:, :, :], qk[u][:, :, :], part[0][u][:, :, :],
                                  ALU.subtract).then_inc(rest_done, 1)

            def scale_v(b, u, n):
                dve.wait_ge(v_done, n + 1)
                dve.wait_ge(stored[u], 16 * (STORES * b + 1))
                dve.tensor_tensor(v_aug[u][:, :, :, :, 0:HEAD_DIM],
                                  v_ps[:, :, :].rearrange("p t (q j d) -> p q t j d", j=QUAD, d=HEAD_DIM),
                                  v_shaped(const.alpha_row), ALU.mult).then_inc(v_scaled, 1)

            def top_norm(b, u, n):
                dve.wait_ge(norms_done, n + 2)
                dve.tensor_reduce(const.top_norms[:, bass.ds(n, 1)], norm_ps, AX.X, ALU.max)\
                    .then_inc(norms_read, 1)

            def first(b, u, n):
                dve.memset(eps[:, :], EPS).then_inc(eps_set, 1)
                statistics(b, u, n)
                normalise(b, u, n)
                statistics(0, 1, 1)
                dve.wait_ge(nat_loaded, 16)
                dve.tensor_reduce(abs_sum[:, :], w_nat[:, :, :], AX.X, ALU.add,
                                  apply_absolute_value=True).then_inc(summed, 1)
                dve.wait_ge(summed, 1)
                dve.tensor_scalar(alpha[:, :], abs_sum[:, :], 1.0 / DIM, None, ALU.mult).then_inc(alpha_done, 1)
                low_of_x(b, u, n)

            def body(blocks):
                if blocks[1]:
                    normalise(*blocks[1])
                if blocks[-2]:
                    top_norm(*blocks[-2])
                if blocks[-1]:
                    rest_of_qk(*blocks[-1])
                    scale_v(*blocks[-1])
                if blocks[2]:
                    statistics(*blocks[2])
                if blocks[1]:
                    low_of_x(*blocks[1])
                if blocks[0] and is_first(blocks[0][2]):
                    dve.wait_ge(alpha_summed, 1)
                    dve.tensor_copy(const.alpha_row[:, :, :], alpha_ps).then_inc(alpha_row_done, 1)
                    dve.wait_ge(alpha_row_done, 1)
                    dve.wait_ge(aug_set, 4)

            steps(dve, first, body)
            dve.wait_ge(norms_read, BLOCKS + 1)
            dve.tensor_reduce(top[:, :], const.top_norms[:, :], AX.X, ALU.max).then_inc(top_done, 1)
            dve.wait_ge(top_turned, 1)
            dve.tensor_reduce(top_qk[:, :], top_ps.rearrange("a (s h) -> a s h", s=2), AX.X,
                              ALU.max).then_inc(top_done, 1)
            dve.wait_ge(top_done, 2)
            dve.tensor_scalar(product[:, :], top_qk[:, 0:1], top_qk[:, 1:2], NORMS_MARGIN, ALU.mult,
                              ALU.mult).then_inc(product_done, 1)
            dve.wait_ge(product_done, 1)
            dve.tensor_scalar(const.wide_range[:, :], product[:, :], NORMS_LIMIT, None, ALU.is_gt)
            dve.wait_ge(bound_spread, 1)
            dve.tensor_scalar(shift[:, :], zeros[:, :], bound_ps, HEADROOM / SCALE, ALU.subtract,
                              ALU.add).then_inc(shift_done, 1)

        @block.gpsimd
        def _(pool):
            pool.memset(ident[:, :], 0.0).then_inc(filled, 1)
            pool.wait_ge(filled, 1)
            pool.affine_select(out=ident[:, :], in_=ident[:, :], compare_op=ALU.not_equal, fill=1.0,
                               base=0, pattern=[[-1, P]], channel_multiplier=1).then_inc(ident_set, 1)
            pool.memset(mean_w[:, :], 1.0 / DIM).then_inc(mean_w_set, 1)
            for u in range(2):
                pool.memset(v_aug[u][:, :, :, :, HEAD_DIM:HEAD_DIM + 1], 1.0).then_inc(aug_set, 1)
                pool.memset(v_aug[u][:, :, :, :, HEAD_DIM + 1:], 0.0).then_inc(aug_set, 1)
            pool.memset(gather[:, :, :], 1.0).then_inc(filled, 1)
            pool.wait_ge(filled, 2)
            pool.affine_select(out=gather[:, :, :], in_=gather[:, :, :], compare_op=ALU.is_ge, fill=0.0,
                               base=0, pattern=[[P, QK], [-HEAD_DIM, 2 * HEADS]],
                               channel_multiplier=1).then_inc(filled, 1)
            pool.wait_ge(filled, 3)
            pool.affine_select(out=gather[:, :, :], in_=gather[:, :, :], compare_op=ALU.is_ge, fill=0.0,
                               base=HEAD_DIM - 1, pattern=[[-P, QK], [HEAD_DIM, 2 * HEADS]],
                               channel_multiplier=-1).then_inc(filled, 1)
            for s in (low_done, rest_done, norms_done, norms_read):
                pool.sem_inc(s, 1)
            for u in range(2):
                pool.sem_inc(stored[u], 16)
            pool.memset(ones[:, :], 1.0).then_inc(bound_set, 1)
            pool.memset(zeros[:, :], 0.0).then_inc(bound_set, 1)
            pool.wait_ge(bound_set, 2)
            for u in range(2):
                pool.memset(quads.k[u][STACK:STACK_M, :, :], 1.0).then_inc(bound_set, 1)
                pool.wait_ge(bound_set, 3 + 2 * u)
                pool.memset(quads.q[u][STACK:STACK_M, :, :], 0.0).then_inc(bound_set, 1)
                pool.wait_ge(bound_set, 4 + 2 * u)
            pool.wait_ge(small_loaded, 16 * 5)
            pool.wait_ge(aug_set, 4)
            with pool.Fori(0, BATCH) as b:
                for u in range(2):
                    n = 2 * b + u
                    pool.wait_ge(mid_done, n + 1)
                    pool.wait_ge(stored[u], 16 * (STORES * b + 1))
                    pool.tensor_tensor(part[2][u][:, :, :], rest[u][:, :, :], part[1][u][:, :, :],
                                       ALU.subtract).then_inc(low_done, 1)
                    pool.wait_ge(v_scaled, n + 1)
                    pool.tensor_tensor(v_aug[u][:, :, :, :, 0:HEAD_DIM], v_aug[u][:, :, :, :, 0:HEAD_DIM],
                                       v_shaped(const.bias_row), ALU.add).then_inc(aug_done, 1)

        @block.scalar
        def _(act):
            def std_of(b, u, n):
                act.wait_ge(var_done, TILES * (n + 1))
                act.activation(std[:, :], mean_var[:, :, 1], ACT.Sqrt, bias=eps[:, :]).then_inc(std_done, 1)

            def high_of_x(b, u, n):
                act.wait_ge(xT_done, n + 1)
                if not isinstance(n, int) or n >= 2:
                    act.wait_ge(v_done, n - 1)
                act.activation(x_hi[u][:, :, :], xT_ps[:, :, :], ACT.Copy).then_inc(hi_done, 1)

            def copy_qk(b, u, n, tiles):
                if not is_first(n):
                    act.wait_ge(rest_done, n)
                for m in tiles:
                    act.wait_ge(qk_done, QK * n + m + 1)
                    act.activation(qk[u][:, m, :], qk_ps[:, m, :], ACT.Identity, bias=bias[:, m:m + 1],
                                   scale=alpha[:, m:m + 1]).then_inc(qk_copied, 1)

            def high_of_qk(b, u, n):
                act.wait_ge(qk_copied, QK * (n + 1))
                act.wait_ge(stored[u], 16 * (STORES * b + 1))
                act.activation(part[0][u][:, :, :], qk[u][:, :, :], ACT.Copy).then_inc(high_done, 1)

            def mid_of_qk(b, u, n):
                act.wait_ge(rest_done, n + 2)
                act.wait_ge(stored[u], 16 * (STORES * b + 1))
                act.activation(part[1][u][:, :, :], rest[u][:, :, :], ACT.Copy).then_inc(mid_done, 1)

            def squares(b, u, n):
                if not is_first(n):
                    act.wait_ge(norms_done, n)
                act.wait_ge(high_done, n + 1)
                act.activation(square[u][:, :, :], part[0][u][:, :, :], ACT.Square).then_inc(square_done, 1)

            def first(b, u, n):
                act.wait_ge(eps_set, 1)
                act.activation(warm[:, :], eps[:, :], ACT.Sqrt)
                std_of(b, u, n)
                std_of(0, 1, 1)
                act.wait_ge(tr_loaded, 16)
                act.activation(signs[:, 0:2, :, :], w_tr[:, 0:2, :, :], ACT.Sign).then_inc(signs_done, 1)
                high_of_x(b, u, n)
                act.wait_ge(tr_v_loaded, 16)
                act.activation(abs_tr[:, :, :, :], w_tr[:, 2:4, :, :], ACT.Abs).then_inc(abs_done, 1)
                act.activation(signs[:, 2:4, :, :], w_tr[:, 2:4, :, :], ACT.Sign).then_inc(signs_done, 1)
                act.wait_ge(alpha_done, 1)
                act.wait_ge(small_loaded, 16 * 5)

            def body(blocks):
                if blocks[0]:
                    copy_qk(*blocks[0], range(0, CT))
                if blocks[1]:
                    high_of_x(*blocks[1])
                if blocks[0]:
                    copy_qk(*blocks[0], range(CT, QK))
                if blocks[2]:
                    std_of(*blocks[2])
                if blocks[-1]:
                    mid_of_qk(*blocks[-1])
                if blocks[0]:
                    high_of_qk(*blocks[0])
                    squares(*blocks[0])

            steps(act, first, body)
            act.wait_ge(product_done, 1)
            act.activation(bound[:, :], product[:, :], ACT.Sqrt).then_inc(root_done, 1)
            act.activation(warm[:, :], eps[:, :], ACT.Exp)

        @block.tensor
        def _(pe):
            def turn_x(b, u, n):
                pe.wait_ge(norm_done, TILES * (n + 1))
                if not is_first(n):
                    pe.wait_ge(lo_done, n)
                    if not isinstance(n, int) or n >= 2:
                        pe.wait_ge(norms_read, n - 1)
                for t in range(TILES):
                    for c in range(CT):
                        i = pe.transpose(xT_ps[:, c, t * P:(t + 1) * P],
                                         x_norm[u][:, t, c * P:(c + 1) * P], ident[:, :])
                i.then_inc(xT_done, 1)

            def project_qk(b, u, n, tiles):
                pe.wait_ge(lo_done, n + 1)
                if is_first(n):
                    pe.wait_ge(signs_done, 1)
                for m in tiles:
                    if not is_first(n):
                        pe.wait_ge(qk_copied, QK * (n - 1) + m + 1)
                    for c in range(CT):
                        w = signs[:, m // CT, c, (m % CT) * P:(m % CT + 1) * P]
                        pe.matmul(qk_ps[:, m, :], w, x_hi[u][:, c, :], start=(c == 0), stop=False)
                        i = pe.matmul(qk_ps[:, m, :], w, x_lo[u][:, c, :], start=False, stop=(c == CT - 1))
                    i.then_inc(qk_done, 1)

            def mean_weights():
                pe.wait_ge(abs_done, 1)
                pe.wait_ge(mean_w_set, 1)
                for c in range(CT):
                    i = pe.matmul(alpha_ps, mean_w[:, :], abs_tr[:, :, c, :], start=(c == 0), stop=(c == CT - 1))
                i.then_inc(alpha_summed, 1)

            def project_v(b, u, n):
                if is_first(n):
                    mean_weights()
                    pe.wait_ge(alpha_row_done, 1)
                    pe.wait_ge(signs_done, 2)
                else:
                    pe.wait_ge(v_scaled, n)
                for t in range(TILES):
                    for c in range(CT):
                        pe.matmul(v_ps[:, t, :], x_hi[u][:, c, t * P:(t + 1) * P], signs[:, 2, c, :],
                                  start=(c == 0), stop=False)
                        i = pe.matmul(v_ps[:, t, :], x_lo[u][:, c, t * P:(t + 1) * P], signs[:, 2, c, :],
                                      start=False, stop=(c == CT - 1))
                i.then_inc(v_done, 1)

            def sum_squares(b, u, n):
                pe.wait_ge(square_done, n + 1)
                pe.wait_ge(norms_read, n + 1)
                for m in range(QK):
                    i = pe.matmul(norm_ps, gather[:, m, :], square[u][:, m, :], start=(m == 0), stop=(m == QK - 1))
                i.then_inc(norms_done, 1)

            def first(b, u, n):
                pe.wait_ge(ident_set, 1)
                turn_x(b, u, n)

            def body(blocks):
                if blocks[-2]:
                    if blocks[0]:
                        pe.wait_ge(lo_done, blocks[0][2] + 1)
                    sum_squares(*blocks[-2])
                if blocks[0]:
                    project_qk(*blocks[0], range(0, CT))
                if blocks[1]:
                    turn_x(*blocks[1])
                if blocks[0]:
                    project_qk(*blocks[0], range(CT, QK))
                    project_v(*blocks[0])
                    if is_first(blocks[0][2]):
                        pe.wait_ge(filled, 4)

            steps(pe, first, body)
            pe.wait_ge(top_done, 1)
            pe.transpose(top_ps, top[:, :], ident[0:2 * HEADS, 0:2 * HEADS]).then_inc(top_turned, 1)
            pe.wait_ge(root_done, 1)
            pe.wait_ge(bound_set, 2)
            pe.matmul(bound_ps, ones[:, :], bound[:, :], start=True, stop=True).then_inc(bound_spread, 1)


def attention(nc, const, q_scr, k_scr, v_scr, m_scr, y_scr, ffn_w, w_scr, W, w_bits, quads, x, tail_in):
    m_rows = m_scr.rearrange("s h (i p) -> (h i) s p", p=P)
    q_st, k_st, v_st, loaded, stored = quads.q, quads.k, quads.v, quads.loaded, quads.stored
    with ExitStack() as ctx:
        def sb(name, shape, dt):
            return ctx.enter_context(nc.sbuf_tensor(name, shape, dt))

        def sem(name):
            return ctx.enter_context(nc.semaphore(name))

        N = QUAD * ST
        probs = [[sb(f"probs{w}{j}", [P, SEQ], F32) for j in range(QUAD)] for w in range(2)]
        y_sb = [sb(f"y_sb{u}", [P, SEQ], F32) for u in range(2)]
        low_bits = sb("low_bits", [P, W_CHUNK], I32)
        row_top = sb("row_top", [P, N], F32)
        neg = [sb(f"neg{s}", [N, P], F32) for s in range(3)]
        m_part = sb("m_part", [N, 3, P], BF16)
        s_ps = [ctx.enter_context(nc.psum_tensor(f"s_ps{i}", [P, SEQ], F32)) for i in range(3)]
        y_ps = ctx.enter_context(nc.psum_tensor("y_ps", [P, SEQ], F32))
        turned_ps = y_ps[0:N, 0:P]
        m_loaded = quads.m_loaded
        mx_m_loaded = sem("mx_m_loaded")
        scored = sem("scored")
        probs_ready = sem("probs_ready")
        pv_done = sem("pv_done")
        y_copied = sem("y_copied")
        y_stored = tail_in.y_stored
        w_in_scr = sem("w_in_scr")
        w_seen = sem("w_seen")
        w_loaded = sem("w_loaded")
        low_bits_done = sem("low_bits_done")
        mx_loaded = sem("mx_loaded")
        mx_scored = sem("mx_scored")
        mx_reduced = sem("mx_reduced")
        mx_turned = sem("mx_turned")
        mx_split = sem("mx_split")
        mx_stored = sem("mx_stored")
        block = ctx.enter_context(nc.Block())

        @block.sync
        def _(sp):
            wide = sp.value_load(const.wide_range[:, :], min_val=0, max_val=1)
            with sp.If(wide):
                for u in range(2):
                    sp.wait_ge(stored[u], 16 * (STORES * BATCH + 1))
                sp.wait_ge(quads.shift_stored, 48)
                sp.wait_ge(loaded[0], 16 * QUAD_LOADS)
                with sp.Fori(0, QUADS) as g:
                    sp.wait_ge(mx_turned, g + 1)
                    load_stacks(sp, q_scr, k_scr, q_st[0], k_st[0], g, mx_loaded)
                    sp.wait_ge(mx_split, 6 * (g + 1) + 1)
                    sp.dma_start(m_rows[bass.ds(g * N, N), :, :], m_part[:, :, :]).then_inc(mx_stored, 16)
                sp.wait_ge(mx_stored, 16 * (QUADS + 1))
                load_stacks(sp, q_scr, k_scr, q_st[0], k_st[0], 0, mx_loaded)
                for u in range(2):
                    sp.dma_start(q_st[u][STACK:STACK_M, :, :],
                                 m_scr[:, u * QUAD:(u + 1) * QUAD, :]).then_inc(mx_m_loaded, 16)

            def load_shift(g, u):
                sp.dma_start(q_st[u][STACK:STACK_M, :, :],
                             m_scr[:, bass.ds(g * QUAD, QUAD), :]).then_inc(m_loaded[u], 16)

            def to_scratch(g):
                sp.dma_start(w_scr[:, bass.ds(g * W_CHUNK, W_CHUNK)],
                             ffn_w[:, bass.ds(g * W_CHUNK, W_CHUNK)]).then_inc(w_in_scr, 16)

            def body(h, last):
                for u in range(2):
                    g = 2 * h + u
                    sp.wait_ge(y_copied, 2 * (g + 1) + 1)
                    sp.dma_start(y_scr[bass.ds(g * P, P), :], y_sb[u][:, :]).then_inc(y_stored[u], 16)
                    if not last:
                        load_quad(sp, q_scr, k_scr, v_scr, quads, g + 2, u)
                        load_shift(g + 2, u)
                    if not (last and u):
                        sp.wait_ge(w_in_scr, 16 * (g + 2))
                        sp.sem_inc(w_seen, 1)
                        sp.dma_start(W[:, bass.ds((g + 1) * W_CHUNK, W_CHUNK)].bitcast(F32),
                                     w_scr[:, bass.ds((g + 1) * W_CHUNK, W_CHUNK)]).then_inc(w_loaded, 16)
                        if not last:
                            to_scratch(g + 2)

            load_quad(sp, q_scr, k_scr, v_scr, quads, 1, 1)
            to_scratch(0)
            for u in range(2):
                sp.wait_ge(stored[u], 16 * (STORES * BATCH + 1))
            sp.wait_ge(quads.shift_stored, 48)
            sp.wait_ge(w_in_scr, 16)
            sp.dma_start(W[:, 0:W_CHUNK].bitcast(F32), w_scr[:, 0:W_CHUNK]).then_inc(w_loaded, 16)
            to_scratch(1)
            with sp.Fori(0, QUADS // 2 - 1) as h:
                body(h, False)
            for u in range(2):
                sp.wait_ge(y_stored[u], 16 * (QUADS // 2))
            load_tail_y(sp, y_scr, tail_in, 0, 0)
            sp.dma_start(tail_in.x1[:, :, :], x_by_block(x)[0]).then_inc(tail_in.x_loaded[0], 16)
            body(QUADS // 2 - 1, True)

        @block.gpsimd
        def _(pool):
            pool.sem_inc(y_copied, 1)
            pool.sem_inc(low_bits_done, 1)
            for s in (mx_turned, mx_split, mx_reduced):
                pool.sem_inc(s, 1)
            pool.sem_inc(mx_stored, 16)
            for u in range(2):
                pool.sem_inc(y_stored[u], 16)

        @block.tensor
        def _(pe):
            wide = pe.value_load(const.wide_range[:, :], min_val=0, max_val=1)
            with pe.If(wide):
                with pe.Fori(0, QUADS) as g:
                    pe.wait_ge(mx_loaded, 16 * 12 * (g + 1))
                    for a in range(N):
                        j, t = divmod(a, ST)
                        pe.wait_ge(mx_reduced, g * N + max(a - 2, 0) + 1)
                        for h in range(2):
                            i = pe.matmul(s_ps[a % 3][:, h * BLK:(h + 1) * BLK],
                                          q_st[0][0:STACK, j, t * P:(t + 1) * P],
                                          k_st[0][0:STACK, j, h * BLK:(h + 1) * BLK], start=True, stop=True)
                        i.then_inc(mx_scored, 1)
                    pe.wait_ge(mx_reduced, (g + 1) * N + 1)
                    pe.wait_ge(mx_split, 6 * g + 1)
                    pe.transpose(turned_ps, row_top[:, :], const.ident[:, :]).then_inc(mx_turned, 1)
                pe.wait_ge(mx_loaded, 16 * 12 * (QUADS + 1))
                pe.wait_ge(mx_m_loaded, 16 * 2)
                pe.wait_ge(mx_split, 6 * QUADS + 1)

            def pv(g, u, s, tb):
                pe.wait_ge(probs_ready, 3 + g * N + QUAD * (s + 1))
                for j in range(QUAD):
                    i = pe.matmul(y_ps[32 * j:32 * (j + 1), tb * BLK:(tb + 1) * BLK],
                                  v_st[u][:, s, 32 * j:32 * (j + 1)],
                                  probs[s % 2][j][:, tb * BLK:(tb + 1) * BLK],
                                  start=(s == 0), stop=(s == ST - 1), tile_position=(0, 32 * j))
                i.then_inc(pv_done, 1)

            def quad(h, u, start):
                g = 2 * h + u
                pe.wait_ge(loaded[u], 16 * QUAD_LOADS * (h + 1))
                pe.wait_ge(m_loaded[u], 16 * (h + 1))
                for s in range(ST):
                    for j in range(QUAD):
                        a = s * QUAD + j
                        pe.wait_ge(probs_ready, g * N + ((2, 3, 1)[a] if a < 3 else a + 1))
                        for tb in range(2):
                            i = pe.matmul(s_ps[a % 3][:, tb * BLK:(tb + 1) * BLK],
                                          k_st[u][:, j, s * P:(s + 1) * P],
                                          q_st[u][:, j, tb * BLK:(tb + 1) * BLK], start=True, stop=True)
                        i.then_inc(scored, 1)
                        if j % 2 and s:
                            if s == 1 and not start:
                                pe.wait_ge(y_copied, 2 * g + j // 2)
                            pv(g, u, s - 1, j // 2)
                        elif j % 2 and not start:
                            pv(g - 1, 1 - u, ST - 1, j // 2)

            quad(0, 0, True)
            quad(0, 1, False)
            with pe.Fori(1, QUADS // 2) as h:
                quad(h, 0, False)
                quad(h, 1, False)
            pv(QUADS - 1, 1, ST - 1, 0)
            pv(QUADS - 1, 1, ST - 1, 1)

        @block.scalar
        def _(act):
            act.sem_inc(pv_done, 4)
            act.sem_inc(probs_ready, 3)
            with act.Fori(0, QUADS // 2) as h:
                for u in range(2):
                    g = 2 * h + u
                    for s in range(ST):
                        act.wait_ge(pv_done, 2 * (g * ST + s + 1))
                        for j in range(QUAD):
                            a = s * QUAD + j
                            act.wait_ge(scored, g * N + a + 1)
                            act.activation(probs[s % 2][j][:, :], s_ps[a % 3][:, :], ACT.Exp,
                                           scale=SCALE).then_inc(probs_ready, 1)

        @block.vector
        def _(dve):
            wide = dve.value_load(const.wide_range[:, :], min_val=0, max_val=1)
            with dve.If(wide):
                with dve.Fori(0, QUADS) as g:
                    dve.wait_ge(mx_turned, g + 1)
                    for a in range(N):
                        dve.wait_ge(mx_scored, g * N + a + 1)
                        dve.tensor_reduce(row_top[:, a:a + 1], s_ps[a % 3][:, :], AX.X,
                                          ALU.max).then_inc(mx_reduced, 1)
                    dve.wait_ge(mx_turned, g + 2)
                    dve.wait_ge(mx_stored, 16 * (g + 1))
                    dve.tensor_scalar(neg[0][:, :], turned_ps, -1.0, None, ALU.mult).then_inc(mx_split, 1)
                    for s in range(3):
                        dve.wait_ge(mx_split, 6 * g + 2 * s + 2)
                        dve.tensor_copy(m_part[:, s, :], neg[s][:, :]).then_inc(mx_split, 1)
                        if s < 2:
                            dve.wait_ge(mx_split, 6 * g + 2 * s + 3)
                            dve.tensor_tensor(neg[s + 1][:, :], neg[s][:, :], m_part[:, s, :],
                                              ALU.subtract).then_inc(mx_split, 1)

            def pair(h):
                for u in range(2):
                    g = 2 * h + u
                    dve.wait_ge(low_bits_done, 2 * g + 1)
                    dve.wait_ge(w_loaded, 16 * (g + 1))
                    dve.tensor_scalar(low_bits[:, :], W[:, bass.ds(g * W_CHUNK, W_CHUNK)].bitcast(I32), LOW_BITS,
                                      None, ALU.bitwise_and).then_inc(low_bits_done, 1)
                    dve.wait_ge(low_bits_done, 2 * g + 2)
                    dve.tensor_reduce(w_bits[:, bass.ds(g, 1)], low_bits[:, :], AX.X, ALU.max)\
                        .then_inc(low_bits_done, 1)
                    dve.wait_ge(y_stored[u], 16 * (h + 1))
                    for tb in range(2):
                        dve.wait_ge(pv_done, 4 + 2 * (g + 1) * ST - 1 + tb)
                        dve.tensor_copy(y_sb[u][:, tb * BLK:(tb + 1) * BLK],
                                        y_ps[:, tb * BLK:(tb + 1) * BLK]).then_inc(y_copied, 1)

            with dve.Fori(0, QUADS // 2 - 1) as h:
                pair(h)
            for part in range(INVERT_PARTS):
                invert_sums(dve, tail_in, 0, part)
            divide_y(dve, tail_in, 0)
            pair(QUADS // 2 - 1)


def tail_ffn(nc, x, y_scr, const, W, w_bits, tail_in, out):
    signs, scales, ident, eps = const.signs, const.scales, const.ident, const.eps
    y, x_loaded, y_done = tail_in.y, tail_in.x_loaded, tail_in.y_done
    x_blk = x_by_block(x)
    o_blk = x_by_block(out)
    with ExitStack() as ctx:
        def sb(name, shape, dt):
            return ctx.enter_context(nc.sbuf_tensor(name, shape, dt))

        def sem(name):
            return ctx.enter_context(nc.semaphore(name))

        x1 = [tail_in.x1, sb("x1_1", [P, TILES, DIM], F32)]
        zn = sb("zn", [P, TILES, DIM], F32)
        x2_hi = sb("x2_hi", [P, CT, BLK], F32R)
        x2_lo = sb("x2_lo", [P, CT, BLK], F32R)
        y_hi, y_lo = x2_hi, x2_lo
        h_hi = [sb(f"h_hi{a}", [P, HT, BLK], F32R) for a in range(2)]
        h_lo = [sb(f"h_lo{a}", [P, HT, BLK], F32R) for a in range(2)]
        gate = [sb(f"gate{a}", [P, BLK], F32) for a in range(3)]
        hid = [sb(f"hid{a}", [P, BLK], F32) for a in range(3)]
        o_sb = zn
        stats = sb("ln_stats", [P, TILES, 6], F32)
        mean_var = sb("ln_mean_var", [P, TILES, 2], F32)
        std = sb("ln_std", [P, TILES], F32)
        rstd = sb("ln_rstd", [P, TILES], F32)
        warm_sqrt = sb("warm_sqrt", [P, 1], F32)
        BANKS = 6
        bank = [ctx.enter_context(nc.psum_tensor(f"ffn_ps{a}", [P, BLK], F32)) for a in range(BANKS)]
        side = ctx.enter_context(nc.psum_tensor("side_ps", [P, CT, BLK], F32))
        side_t = side[:, :, :].rearrange("p a (t c) -> p (a t) c", c=DIM)

        bits_ps = bank[0][0:1, 0:P]

        def row_by_tile(row, tiles):
            return row.unsqueeze(1).to_broadcast([P, tiles, DIM])

        def is_first(n):
            return isinstance(n, int) and n == 0

        top_row_bits = sb("top_row_bits", [P, 1], F32)
        any_low = sb("any_low", [1, 1], I32)
        top_bits = sb("top_bits", [1, 1], F32)
        bits_done = sem("bits_done")
        bits_turned = sem("bits_turned")
        y_hi_done = sem("y_hi_done")
        y_lo_done = sem("y_lo_done")
        proj_done = sem("proj_done")
        z_scaled = sem("z_scaled")
        z_done = sem("z_done")
        zn_done = sem("zn_done")
        x1_done = sem("x1_done")
        x1n_done = sem("x1n_done")
        x2T_done = sem("x2T_done")
        x2_hi_done = sem("x2_hi_done")
        x2_lo_done = sem("x2_lo_done")
        ln_stats_done = sem("ln_stats_done")
        ln_stats_seen = sem("ln_stats_seen")
        ln_var_done = sem("ln_var_done")
        ln_std_done = sem("ln_std_done")
        ln_rstd_done = sem("ln_rstd_done")
        tile_done = sem("tile_done")
        gate_done = sem("gate_done")
        prod_done = sem("prod_done")
        hi1_done = sem("hi1_done")
        gelu_done = sem("gelu_done")
        hi2_done = sem("hi2_done")
        h_lo_done = sem("h_lo_done")
        o_scaled = sem("o_scaled")
        o_norm = sem("o_norm")
        o_done = sem("o_done")
        o_stored = sem("o_stored")

        kinds = ["gate", "prod"] * HT + ["gelu"] * (2 * HT) + ["out"] * CT
        NT = len(kinds)
        reader = {"gate": gate_done, "prod": prod_done, "gelu": gelu_done, "out": o_scaled}
        per_block = {k: kinds.count(k) for k in reader}
        L2_AT, L3_AT, OUT_AT = 2 * HT, 3 * HT, 4 * HT

        def bank_of(t):
            return bank[t % BANKS]

        def wait_bank(pe, i, t):
            if t >= BANKS:
                before, blk = t - BANKS, i
            else:
                before, blk = max(p for p in range(NT) if p % BANKS == t), i - 1
                if isinstance(i, int) and i == 0:
                    return
            k = kinds[before]
            pe.wait_ge(reader[k], per_block[k] * blk + kinds[:before + 1].count(k))

        def ln_z(t):
            return 3 * t - 1 if not isinstance(t, int) or t else 0

        def ln_x1(t):
            return 3 * t if not isinstance(t, int) or t else 1

        def ln_out(f):
            return 3 * f + 4 if not isinstance(f, int) or f < BLOCKS - 1 else 3 * f + 2

        block = ctx.enter_context(nc.Block())

        def blocks(eng, step, end):
            step(0, 0, (0, 1), None)
            with eng.Fori(0, BATCH - 1) as b:
                step(2 * b + 1, 1, (b + 1, 0), (b, 0))
                step(2 * b + 2, 0, (b + 1, 1), (b, 1))
            step(BLOCKS - 1, 1, None, (BATCH - 1, 0))
            end()

        @block.sync
        def _(sp):
            def load_y(t, b, u):
                sp.wait_ge(y_lo_done, t)
                load_tail_y(sp, y_scr, tail_in, b, u)

            def load_x(t, u):
                if not isinstance(t, int) or t >= 2:
                    sp.wait_ge(o_done, t - 1)
                sp.dma_start(x1[u][:, :, :], x_blk[t]).then_inc(x_loaded[u], 16)

            def store(f):
                sp.wait_ge(o_done, f + 1)
                sp.dma_start(o_blk[f], o_sb[:, :, :]).then_inc(o_stored, 16)

            def step(i, u, ahead, behind):
                if ahead:
                    load_y(i + 1, *ahead)
                if behind:
                    store(i - 1)
                if ahead:
                    load_x(i + 1, 1 - u)

            for u in range(2):
                sp.wait_ge(tail_in.y_stored[u], 16 * (QUADS // 2 + 1))
            blocks(sp, step, lambda: store(BLOCKS - 1))
            sp.wait_ge(o_stored, 16 * BLOCKS)

        @block.tensor
        def _(pe):
            def project_y(t):
                pe.wait_ge(y_hi_done, t + 1)
                pe.wait_ge(y_lo_done, t + 1)
                pe.wait_ge(x2_lo_done, t)
                for a in range(TILES):
                    for c in range(CT):
                        for y_part in (y_hi, y_lo):
                            i = pe.matmul(side_t[:, a, :], y_part[:, c, a * P:(a + 1) * P], signs[:, 3, c, :],
                                          start=(c == 0 and y_part is y_hi),
                                          stop=(c == CT - 1 and y_part is y_lo))
                i.then_inc(proj_done, 1)

            def turn_x1(t):
                pe.wait_ge(x1n_done, TILES * (t + 1))
                for a in range(TILES):
                    for c in range(CT):
                        i = pe.transpose(side[:, c, a * P:(a + 1) * P], zn[:, a, c * P:(c + 1) * P], ident[:, :])
                i.then_inc(x2T_done, 1)

            def tile(i, t, w_at, width, m, chunks, hi, lo):
                for k, last in chunks:
                    w = W[:, w_at + k * width + m * P:w_at + k * width + (m + 1) * P].bitcast(form)
                    pe.matmul(bank_of(t)[:, :], w, hi[:, k, :].bitcast(form), start=(k == 0), stop=False)
                    mm = pe.matmul(bank_of(t)[:, :], w, lo[:, k, :].bitcast(form), start=False, stop=last)
                    if last:
                        mm.then_inc(tile_done, 1)

            def wide(i, t0, w_at, width, ms, hi, lo, done_before):
                for k in range(HT):
                    if done_before is not None:
                        pe.wait_ge(h_lo_done, done_before + k + 1)
                    for m in ms:
                        if k == 0:
                            wait_bank(pe, i, t0 + m)
                        tile(i, t0 + m, w_at, width, m, [(k, k == HT - 1)], hi, lo)

            def out_tiles(i, hi, lo):
                per_bank = TILES // CT
                for k in range(HT):
                    pe.wait_ge(h_lo_done, 3 * HT * i + 2 * HT + k + 1)
                    w = W[:, W3_AT + k * DIM:W3_AT + (k + 1) * DIM].bitcast(form)
                    for m in range(CT):
                        if k == 0:
                            wait_bank(pe, i, OUT_AT + m)
                        for a in range(per_bank):
                            tokens = slice((m * per_bank + a) * P, (m * per_bank + a + 1) * P)
                            dst = bank_of(OUT_AT + m)[:, a * DIM:(a + 1) * DIM]
                            pe.matmul(dst, hi[:, k, tokens].bitcast(form), w, start=(k == 0 and a == 0), stop=False)
                            mm = pe.matmul(dst, lo[:, k, tokens].bitcast(form), w, start=False,
                                           stop=(k == HT - 1 and a == per_bank - 1))
                        if k == HT - 1:
                            mm.then_inc(tile_done, 1)

            def step(i, u, ahead, behind):
                pe.wait_ge(x2_lo_done, i + 1)
                for n in range(HT):
                    for a, w_at in ((0, W1_AT), (1, W2_AT)):
                        wait_bank(pe, i, 2 * n + a)
                        tile(i, 2 * n + a, w_at, HIDDEN, n, [(0, False), (1, True)], x2_hi, x2_lo)
                t = i + 1
                wide(i, L2_AT, H1_AT, HIDDEN, (0, 1, 2), h_hi[0], h_lo[0], 3 * HT * i)
                wide(i, L2_AT, H1_AT, HIDDEN, (3, 4, 5), h_hi[0], h_lo[0], None)
                wide(i, L2_AT, H1_AT, HIDDEN, (6, 7), h_hi[0], h_lo[0], None)
                if ahead:
                    project_y(t)
                wide(i, L3_AT, H2_AT, HIDDEN, (0, 1, 2), h_hi[1], h_lo[1], 3 * HT * i + HT)
                wide(i, L3_AT, H2_AT, HIDDEN, (3, 4, 5), h_hi[1], h_lo[1], None)
                wide(i, L3_AT, H2_AT, HIDDEN, (6, 7), h_hi[1], h_lo[1], None)
                if ahead:
                    turn_x1(t)
                out_tiles(i, h_hi[0], h_lo[0])

            pe.wait_ge(bits_done, 1)
            pe.transpose(bits_ps, top_row_bits[:, :], ident[:, :]).then_inc(bits_turned, 1)
            project_y(0)
            turn_x1(0)
            pe.wait_ge(bits_done, 3)
            inexact = pe.value_load(any_low[:, :], min_val=0, max_val=1)
            with pe.If(inexact):
                form = F32
                blocks(pe, step, lambda: None)
            with pe.Else():
                form = F32R
                blocks(pe, step, lambda: None)

        @block.scalar
        def _(act):
            def ln_std(n):
                act.wait_ge(ln_var_done, TILES * (n + 1))
                act.activation(std[:, :], mean_var[:, :, 1], ACT.Sqrt, bias=eps[:, :]).then_inc(ln_std_done, 1)

            def high_of_y(t):
                act.wait_ge(y_done, t + 1)
                act.wait_ge(proj_done, t)
                act.activation(y_hi[:, :, :], y[:, :, :], ACT.Copy).then_inc(y_hi_done, 1)

            def high_of_x1(t):
                act.wait_ge(x2T_done, t + 1)
                act.activation(x2_hi[:, :, :], side[:, :, :], ACT.Copy).then_inc(x2_hi_done, 1)

            def high_of_hidden(i, n):
                act.wait_ge(prod_done, HT * i + n + 1)
                act.activation(h_hi[0][:, n, :], hid[n % 3][:, :], ACT.Copy).then_inc(hi1_done, 1)

            def gelu(i, layer, n):
                t = (L2_AT if layer == 0 else L3_AT) + n
                s = (SH1_AT if layer == 0 else SH2_AT) + n
                act.wait_ge(tile_done, NT * i + t + 1)
                done = 3 * HT * i + HT * (layer + 1) + n
                act.wait_ge(h_lo_done, done - 2)
                act.activation(hid[n % 3][:, :], bank_of(t)[:, :], ACT.Gelu,
                               scale=scales[:, s:s + 1]).then_inc(gelu_done, 1)

            def step(i, u, ahead, behind):
                t = i + 1
                for n in range(HT):
                    act.wait_ge(tile_done, NT * i + 2 * n + 1)
                    if n >= 3:
                        act.wait_ge(prod_done, HT * i + n - 2)
                    else:
                        act.wait_ge(prod_done, HT * i)
                    act.activation(gate[n % 3][:, :], bank_of(2 * n)[:, :], ACT.Silu,
                                   scale=scales[:, S1_AT + n:S1_AT + n + 1]).then_inc(gate_done, 1)
                    if n:
                        high_of_hidden(i, n - 1)
                high_of_hidden(i, HT - 1)
                if behind:
                    ln_std(ln_out(i - 1))
                for n in range(HT):
                    gelu(i, 0, n)
                    if n == 3 and ahead:
                        high_of_y(t)
                if ahead:
                    ln_std(ln_z(t))
                    ln_std(ln_x1(t))
                for n in range(HT):
                    gelu(i, 1, n)
                if ahead:
                    high_of_x1(t)

            def end():
                ln_std(ln_out(BLOCKS - 1))

            high_of_y(0)
            act.activation(warm_sqrt[:, :], eps[:, :], ACT.Sqrt)
            ln_std(ln_z(0))
            ln_std(ln_x1(0))
            high_of_x1(0)
            blocks(act, step, end)

        @block.vector
        def _(dve):
            def ln_stats(n, src):
                for a in range(TILES):
                    dve.bn_stats(stats[:, a, :], src[:, a, :]).then_inc(ln_stats_done, 1)
                dve.wait_ge(ln_stats_done, TILES * (n + 1))
                dve.sem_inc(ln_stats_seen, 1)
                for a in range(TILES):
                    dve.bn_aggr(mean_var[:, a, :], stats[:, a, :]).then_inc(ln_var_done, 1)

            def ln_norm(n, dst, src, done):
                dve.wait_ge(ln_std_done, n + 1)
                dve.reciprocal(rstd[:, :], std[:, :]).then_inc(ln_rstd_done, 1)
                dve.wait_ge(ln_rstd_done, n + 1)
                for a in range(TILES):
                    dve.tensor_scalar(dst[:, a, :], src[:, a, :], mean_var[:, a, 0:1], rstd[:, a:a + 1],
                                      ALU.subtract, ALU.mult).then_inc(done, 1)

            def low_of_y(t):
                dve.wait_ge(y_hi_done, t + 1)
                dve.tensor_tensor(y_lo[:, :, :], y[:, :, :], y_hi[:, :, :].bitcast(F32),
                                  ALU.subtract).then_inc(y_lo_done, 1)

            def residual(t, b, u):
                dve.wait_ge(proj_done, t + 1)
                dve.wait_ge(x2T_done, t)
                if not isinstance(t, int) or t >= 2:
                    dve.wait_ge(o_stored, 16 * (t - 1))
                dve.tensor_tensor(zn[:, :, :], side_t, row_by_tile(const.alpha_row[:, 1, :], TILES),
                                  ALU.mult).then_inc(z_scaled, 1)
                dve.wait_ge(z_scaled, t + 1)
                dve.tensor_tensor(zn[:, :, :], zn[:, :, :], row_by_tile(const.bias_row[:, 1, :], TILES),
                                  ALU.add).then_inc(z_done, 1)
                dve.wait_ge(z_done, t + 1)
                ln_stats(ln_z(t), zn)
                ln_norm(ln_z(t), zn, zn, zn_done)
                dve.wait_ge(zn_done, TILES * (t + 1))
                dve.wait_ge(x_loaded[u], 16 * (b + 1))
                dve.tensor_tensor(x1[u][:, :, :], x1[u][:, :, :], zn[:, :, :], ALU.add).then_inc(x1_done, 1)
                dve.wait_ge(x1_done, t + 1)
                ln_stats(ln_x1(t), x1[u])
                ln_norm(ln_x1(t), zn, x1[u], x1n_done)

            def low_of_x1(t):
                dve.wait_ge(x2_hi_done, t + 1)
                dve.tensor_tensor(x2_lo[:, :, :], side[:, :, :], x2_hi[:, :, :].bitcast(F32),
                                  ALU.subtract).then_inc(x2_lo_done, 1)

            def scale_out(f, ahead):
                dve.wait_ge(x2T_done, f + 2 if ahead else BLOCKS)
                if not is_first(f):
                    dve.wait_ge(o_stored, 16 * f)
                for m in range(CT):
                    dve.wait_ge(tile_done, NT * f + OUT_AT + m + 1)
                    tiles = slice(m * (TILES // CT), (m + 1) * (TILES // CT))
                    dve.tensor_tensor(o_sb[:, tiles, :],
                                      bank_of(OUT_AT + m)[:, :].rearrange("p (t c) -> p t c", c=DIM),
                                      row_by_tile(const.out_row[:, :], TILES // CT), ALU.mult)\
                        .then_inc(o_scaled, 1)

            def finish_out(f, u):
                dve.wait_ge(o_scaled, CT * (f + 1))
                ln_stats(ln_out(f), o_sb)
                ln_norm(ln_out(f), o_sb, o_sb, o_norm)
                dve.wait_ge(o_norm, TILES * (f + 1))
                dve.tensor_tensor(o_sb[:, :, :], o_sb[:, :, :], x1[u][:, :, :], ALU.add).then_inc(o_done, 1)

            def low_of_hidden(i, layer, n):
                a = 0 if layer != 1 else 1
                if layer == 0:
                    dve.wait_ge(hi1_done, HT * i + n + 1)
                else:
                    dve.wait_ge(hi2_done, 2 * HT * i + HT * (layer - 1) + n + 1)
                dve.tensor_tensor(h_lo[a][:, n, :], hid[n % 3][:, :], h_hi[a][:, n, :].bitcast(F32),
                                  ALU.subtract).then_inc(h_lo_done, 1)

            def high_of_hidden(i, layer, n):
                a = 0 if layer != 1 else 1
                dve.wait_ge(gelu_done, 2 * HT * i + HT * (layer - 1) + n + 1)
                dve.tensor_copy(h_hi[a][:, n, :], hid[n % 3][:, :]).then_inc(hi2_done, 1)

            def step(i, u, ahead, behind):
                t = i + 1
                for n in range(HT):
                    dve.wait_ge(gate_done, HT * i + n + 1)
                    dve.wait_ge(tile_done, NT * i + 2 * n + 2)
                    dve.wait_ge(h_lo_done, 3 * HT * i + n - 2 if n > 2 else 3 * HT * i)
                    dve.scalar_tensor_tensor(hid[n % 3][:, :], bank_of(2 * n + 1)[:, :],
                                             scales[:, S2_AT + n:S2_AT + n + 1], gate[n % 3][:, :],
                                             ALU.mult, ALU.mult).then_inc(prod_done, 1)
                    if n:
                        low_of_hidden(i, 0, n - 1)
                low_of_hidden(i, 0, HT - 1)
                if behind:
                    finish_out(i - 1, 1 - u)
                if ahead:
                    for part in range(INVERT_PARTS // 2):
                        invert_sums(dve, tail_in, t, part)
                for layer in (1, 2):
                    for n in range(HT):
                        high_of_hidden(i, layer, n)
                        if n:
                            low_of_hidden(i, layer, n - 1)
                        if layer == 1 and ahead:
                            if n < INVERT_PARTS // 2:
                                invert_sums(dve, tail_in, t, INVERT_PARTS // 2 + n)
                            elif n == INVERT_PARTS // 2:
                                divide_y(dve, tail_in, t)
                            elif n == 5:
                                low_of_y(t)
                    low_of_hidden(i, layer, HT - 1)
                    if layer == 2 and ahead:
                        low_of_x1(t)
                    if layer == 1 and ahead:
                        residual(t, *ahead)
                scale_out(i, ahead)

            dve.tensor_reduce(top_row_bits[:, :], w_bits[:, :], AX.X, ALU.max).then_inc(bits_done, 1)
            low_of_y(0)
            dve.wait_ge(bits_turned, 1)
            dve.tensor_reduce(top_bits[:, :], bits_ps, AX.X, ALU.max).then_inc(bits_done, 1)
            dve.wait_ge(bits_done, 2)
            dve.tensor_scalar(any_low[:, :], top_bits[:, :], 0.0, None, ALU.is_gt).then_inc(bits_done, 1)
            residual(0, 0, 0)
            low_of_x1(0)
            blocks(dve, step, lambda: finish_out(BLOCKS - 1, (BLOCKS - 1) % 2))


def kernel(L0_attn_x, L0_attn_Wq, L0_attn_bq, L0_attn_Wk, L0_attn_bk, L0_attn_Wv, L0_attn_bv, L0_attn_Wp,
           L0_attn_bp, L0_ffn_w1_w, L0_ffn_w1_s, L0_ffn_w2_w, L0_ffn_w2_s, L0_ffn_h1_w, L0_ffn_h1_s,
           L0_ffn_h2_w, L0_ffn_h2_s, L0_ffn_w3_w, L0_ffn_w3_s):
    import numpy as np
    import concourse.bacc as bacc
    from concourse.bass_utils import run_bass_kernel_spmd

    def rows(a):
        return a.reshape(-1, P, a.shape[-1]).transpose(1, 0, 2)

    attn = [np.asarray(a) for a in (L0_attn_Wq, L0_attn_Wk, L0_attn_Wv, L0_attn_Wp)]
    attn_b = [np.asarray(a) for a in (L0_attn_bq, L0_attn_bk, L0_attn_bv, L0_attn_bp)]
    ffn = [np.asarray(a) for a in (L0_ffn_w1_w, L0_ffn_w2_w, L0_ffn_h1_w, L0_ffn_h2_w, L0_ffn_w3_w)]
    ffn_s = [np.asarray(a) for a in (L0_ffn_w1_s, L0_ffn_w2_s, L0_ffn_h1_s, L0_ffn_h2_s, L0_ffn_w3_s)]
    arrays = {
        "x": np.asarray(L0_attn_x),
        "attn_w": rows(np.concatenate(attn[:2])),
        "attn_wT": np.stack([rows(a.T) for a in attn], axis=1),
        "attn_b": np.concatenate(attn_b[:2]).reshape(-1, P).T,
        "attn_b_rows": np.stack(attn_b[2:]),
        "ffn_w": np.concatenate([rows(a.T).reshape(P, -1) for a in ffn], axis=1),
        "ffn_s": np.concatenate(ffn_s[:4]).reshape(-1, P).T,
        "ffn_s3": ffn_s[4].reshape(-1),
    }
    arrays = {name: np.ascontiguousarray(a) for name, a in arrays.items()}
    nc = bacc.Bacc("TRN2", target_bir_lowering=False, num_devices=1)
    ins = {name: nc.dram_tensor(name, a.shape, mybir.dt.from_np(a.dtype), kind="ExternalInput").ap()
           for name, a in arrays.items()}
    out = nc.dram_tensor("out", (BATCH, SEQ, DIM), F32, kind="ExternalOutput").ap()
    layer(nc, out=out, **ins)
    r = run_bass_kernel_spmd(nc, [arrays], core_ids=[0])
    return r.results[0]["out"]
```
